# Optimizing a Trainium2 kernel written in Bass

```python
import numpy as np
import jax
import jax.numpy as jnp

def _softmax(x, axis=-1):
    return jax.nn.softmax(x, axis=axis)

def _gelu(x):
    return jax.nn.gelu(x, approximate=True)

def _silu(x):
    return jax.nn.silu(x)

def _sigmoid(x):
    return jax.nn.sigmoid(x)

def _layernorm(x, axis=-1, eps=1e-05):
    m = jnp.mean(x, axis=axis, keepdims=True)
    v = jnp.var(x, axis=axis, keepdims=True)
    return (x - m) / jnp.sqrt(v + eps)

def _scatter_add(tgt, idx, src, axis=0):
    return tgt.at[idx].add(src)

def _segment_sum(src, seg, n):
    return jax.ops.segment_sum(src, seg, n)
kernel_name = 'mk_decoder_preln_d1_seqx_r4_9ad3fe'

def setup_inputs(seed: int=0):
    np.random.seed(seed)
    _w = jnp.asarray

    def _rec_inputs():
        import jax
        import jax.numpy as jnp
        _rk = jax.random.key(seed)
        x = -0.0003929 + 0.9999 * jax.random.normal(jax.random.fold_in(_rk, 1), (16, 128, 256), jnp.float32)
        _lenS = 128 - jax.random.randint(jax.random.fold_in(_rk, 7), (16,), 0, max(1, 128 // 4) + 1, jnp.int32)
        _lenS2 = 128 - jax.random.randint(jax.random.fold_in(_rk, 8), (16,), 0, max(1, 128 // 4) + 1, jnp.int32)
        _ctx_1024P = jax.random.normal(jax.random.fold_in(_rk, 11), (16, 16, 256), jnp.float32)
        _ctx_1024c = jax.random.dirichlet(jax.random.fold_in(_rk, 511), 0.3 * jnp.ones((16,), jnp.float32), (16, 128))
        _ctx_1024t = jnp.einsum('bsk,bkd->bsd', _ctx_1024c, _ctx_1024P)
        _ctx_1024t = _ctx_1024t * jax.lax.rsqrt(jnp.mean(jnp.square(_ctx_1024t)) + 1e-12) * 0.953939
        ctx_1024 = 2.81802e-05 + 1.00001 * (_ctx_1024t + 0.3 * jax.random.normal(jax.random.fold_in(_rk, 611), (16, 128, 256), jnp.float32))
        return (x, ctx_1024)
    x, ctx_1024 = _rec_inputs()

    def _L0_attn_setup():
        import jax, jax.numpy as jnp
        import numpy as np
        B, T, C = (2, 512, 256)
        H, L = (16, 72)
        D_HEAD = C // H
        key = jax.random.key(seed)
        ks = jax.random.split(key, 7)
        s = 0.02
        return {'x': jax.random.normal(ks[0], (B, T, C), dtype=jnp.float32), 'latent_w': jax.random.normal(ks[1], (C, L), dtype=jnp.float32) * s, 'latent_b': jax.random.normal(ks[2], (L,), dtype=jnp.float32) * s, 'Wd_w': jax.random.normal(ks[3], (H, C, L), dtype=jnp.float32) * s, 'Wd_b': jax.random.normal(ks[4], (H, L), dtype=jnp.float32) * s, 'out_w': jax.random.normal(ks[5], (H * L, C), dtype=jnp.float32) * s, 'out_b': jax.random.normal(ks[6], (C,), dtype=jnp.float32) * s}
    _L0_attn_all = _L0_attn_setup()
    _L0_attn_in = {k: v for k, v in _L0_attn_all.items() if k in ('latent_w', 'latent_b', 'Wd_w', 'Wd_b', 'out_w', 'out_b')}
    del _L0_attn_all

    def _L0_xattn_setup():
        import jax, jax.numpy as jnp
        import numpy as np
        B_SZ, T_LEN, C_DIM = (4, 1024, 256)

        def _wkv_scan(ek, v, ew):

            def step(carry, xt):
                A, Bd = carry
                ekt, vt = xt
                out = (A, Bd)
                A2 = ew * A + ekt * vt
                B2 = ew * Bd + ekt
                return ((A2, B2), out)
            init = (jnp.zeros_like(ek[:, 0]), jnp.zeros_like(ek[:, 0]))
            xs = (jnp.moveaxis(ek, 1, 0), jnp.moveaxis(v, 1, 0))
            _, (A, Bd) = jax.lax.scan(step, init, xs)
            return (jnp.moveaxis(A, 0, 1), jnp.moveaxis(Bd, 0, 1))

        def _birwkv(r, k, v, w, u):
            wc = w.reshape(-1)
            uc = u.reshape(-1)
            ew = jnp.exp(wc)
            ek = jnp.exp(k)
            Af, Bf = _wkv_scan(ek, v, ew)
            Ab, Bb = _wkv_scan(ek[:, ::-1], v[:, ::-1], ew)
            Ab = Ab[:, ::-1]
            Bb = Bb[:, ::-1]
            cur = jnp.exp(uc + k)
            wkv = (Af + Ab + cur * v) / (Bf + Bb + cur)
            return jax.nn.sigmoid(r) * wkv
        key = jax.random.key(seed)
        k1, k2, k3, k4, k5 = jax.random.split(key, 5)
        r = jax.random.normal(k1, (B_SZ, T_LEN, C_DIM), dtype=jnp.float32)
        k = jax.random.normal(k2, (B_SZ, T_LEN, C_DIM), dtype=jnp.float32)
        v = jax.random.normal(k3, (B_SZ, T_LEN, C_DIM), dtype=jnp.float32)
        w = -(0.3 + jax.random.uniform(k4, (1, 1, C_DIM), dtype=jnp.float32))
        u = jax.random.normal(k5, (1, 1, C_DIM), dtype=jnp.float32) * 0.1
        return {'r': r, 'k': k, 'v': v, 'w': w, 'u': u}
    _L0_xattn_all = _L0_xattn_setup()
    _L0_xattn_in = {k: v for k, v in _L0_xattn_all.items() if k in ('w', 'u')}
    del _L0_xattn_all

    def _L0_ffn_setup():
        import jax, jax.numpy as jnp
        import numpy as np
        JITTER_EPS = 0.01
        NEG_INF = -jnp.inf

        def sparsemixer_eval(scores, jitter_eps):
            m1 = jnp.max(scores, axis=-1, keepdims=True)
            ind1 = jnp.argmax(scores, axis=-1)
            factor1 = jnp.maximum(jnp.abs(scores), m1)
            mask1 = jax.lax.stop_gradient((m1 - scores) / factor1 > 2.0 * jitter_eps)
            gates1 = jax.nn.softmax(jnp.where(mask1, NEG_INF, scores), axis=-1)
            mult1 = jnp.take_along_axis(gates1, ind1[:, None], axis=-1)[:, 0]
            E = scores.shape[-1]
            onehot1 = ind1[:, None] == jnp.arange(E)[None, :]
            masked_scores = jnp.where(onehot1, NEG_INF, scores)
            m2 = jnp.max(masked_scores, axis=-1, keepdims=True)
            ind2 = jnp.argmax(masked_scores, axis=-1)
            factor2 = jnp.maximum(jnp.abs(scores), m2)
            mask2 = jax.lax.stop_gradient((m2 - scores) / factor2 > 2.0 * jitter_eps)
            gates2 = jax.nn.softmax(jnp.where(mask2, NEG_INF, masked_scores), axis=-1)
            mult2 = jnp.take_along_axis(gates2, ind2[:, None], axis=-1)[:, 0]
            multiplier = jnp.stack([mult1, mult2], axis=-1)
            selected = jnp.stack([ind1, ind2], axis=-1)
            return (multiplier, selected)
        key = jax.random.key(seed)
        k0, k1, k2, k3, k4 = jax.random.split(key, 5)
        B, S, H, F, E = (2, 256, 256, 512, 8)
        scale = 0.02
        return {'hidden_states': jax.random.normal(k0, (B, S, H), dtype=jnp.float32), 'router_w': jax.random.normal(k1, (E, H), dtype=jnp.float32) * scale, 'w_gate': jax.random.normal(k2, (E, F, H), dtype=jnp.float32) * scale, 'w_up': jax.random.normal(k3, (E, F, H), dtype=jnp.float32) * scale, 'w_down': jax.random.normal(k4, (E, H, F), dtype=jnp.float32) * scale}
    _L0_ffn_all = _L0_ffn_setup()
    _L0_ffn_in = {k: v for k, v in _L0_ffn_all.items() if k in ('router_w', 'w_gate', 'w_up', 'w_down')}
    del _L0_ffn_all
    return {'x': x, 'ctx_1024': ctx_1024, 'L0_attn_latent_w': _L0_attn_in['latent_w'], 'L0_attn_latent_b': _L0_attn_in['latent_b'], 'L0_attn_Wd_w': _L0_attn_in['Wd_w'], 'L0_attn_Wd_b': _L0_attn_in['Wd_b'], 'L0_attn_out_w': _L0_attn_in['out_w'], 'L0_attn_out_b': _L0_attn_in['out_b'], 'L0_xattn_w': _L0_xattn_in['w'], 'L0_xattn_u': _L0_xattn_in['u'], 'L0_ffn_router_w': _L0_ffn_in['router_w'], 'L0_ffn_w_gate': _L0_ffn_in['w_gate'], 'L0_ffn_w_up': _L0_ffn_in['w_up'], 'L0_ffn_w_down': _L0_ffn_in['w_down']}

def reference(x, ctx_1024, L0_attn_latent_w, L0_attn_latent_b, L0_attn_Wd_w, L0_attn_Wd_b, L0_attn_out_w, L0_attn_out_b, L0_xattn_w, L0_xattn_u, L0_ffn_router_w, L0_ffn_w_gate, L0_ffn_w_up, L0_ffn_w_down):
    import jax
    import jax.numpy as jnp

    def _L0_attn_ref(x, latent_w, latent_b, Wd_w, Wd_b, out_w, out_b):
        import jax, jax.numpy as jnp
        import numpy as np
        B, T, C = (2, 512, 256)
        H, L = (16, 72)
        D_HEAD = C // H
        b, t, c = x.shape
        h = Wd_w.shape[0]
        d_head = c // h
        Wdkv = x @ latent_w + latent_b
        q = jnp.einsum('btc,hcl->bhtl', x, Wd_w) + Wd_b[None, :, None, :]
        scores = jnp.einsum('bhtl,bsl->bhts', q, Wdkv) / jnp.asarray(np.sqrt(d_head), dtype=x.dtype)
        causal = jnp.tril(jnp.ones((t, t), dtype=bool))
        scores = jnp.where(causal[None, None, :, :], scores, -jnp.inf)
        attn = jax.nn.softmax(scores, axis=-1)
        y = jnp.einsum('bhts,bsl->bhtl', attn, Wdkv)
        z = jnp.transpose(y, (0, 2, 1, 3)).reshape(b, t, h * Wdkv.shape[-1])
        return z @ out_w + out_b

    def _L0_xattn_ref(r, k, v, w, u):
        import jax, jax.numpy as jnp
        import numpy as np
        B_SZ, T_LEN, C_DIM = (4, 1024, 256)

        def _wkv_scan(ek, v, ew):

            def step(carry, xt):
                A, Bd = carry
                ekt, vt = xt
                out = (A, Bd)
                A2 = ew * A + ekt * vt
                B2 = ew * Bd + ekt
                return ((A2, B2), out)
            init = (jnp.zeros_like(ek[:, 0]), jnp.zeros_like(ek[:, 0]))
            xs = (jnp.moveaxis(ek, 1, 0), jnp.moveaxis(v, 1, 0))
            _, (A, Bd) = jax.lax.scan(step, init, xs)
            return (jnp.moveaxis(A, 0, 1), jnp.moveaxis(Bd, 0, 1))

        def _birwkv(r, k, v, w, u):
            wc = w.reshape(-1)
            uc = u.reshape(-1)
            ew = jnp.exp(wc)
            ek = jnp.exp(k)
            Af, Bf = _wkv_scan(ek, v, ew)
            Ab, Bb = _wkv_scan(ek[:, ::-1], v[:, ::-1], ew)
            Ab = Ab[:, ::-1]
            Bb = Bb[:, ::-1]
            cur = jnp.exp(uc + k)
            wkv = (Af + Ab + cur * v) / (Bf + Bb + cur)
            return jax.nn.sigmoid(r) * wkv
        return _birwkv(r, k, v, w, u)

    def _L0_ffn_ref(hidden_states, router_w, w_gate, w_up, w_down):
        import jax, jax.numpy as jnp
        import numpy as np
        JITTER_EPS = 0.01
        NEG_INF = -jnp.inf

        def sparsemixer_eval(scores, jitter_eps):
            m1 = jnp.max(scores, axis=-1, keepdims=True)
            ind1 = jnp.argmax(scores, axis=-1)
            factor1 = jnp.maximum(jnp.abs(scores), m1)
            mask1 = jax.lax.stop_gradient((m1 - scores) / factor1 > 2.0 * jitter_eps)
            gates1 = jax.nn.softmax(jnp.where(mask1, NEG_INF, scores), axis=-1)
            mult1 = jnp.take_along_axis(gates1, ind1[:, None], axis=-1)[:, 0]
            E = scores.shape[-1]
            onehot1 = ind1[:, None] == jnp.arange(E)[None, :]
            masked_scores = jnp.where(onehot1, NEG_INF, scores)
            m2 = jnp.max(masked_scores, axis=-1, keepdims=True)
            ind2 = jnp.argmax(masked_scores, axis=-1)
            factor2 = jnp.maximum(jnp.abs(scores), m2)
            mask2 = jax.lax.stop_gradient((m2 - scores) / factor2 > 2.0 * jitter_eps)
            gates2 = jax.nn.softmax(jnp.where(mask2, NEG_INF, masked_scores), axis=-1)
            mult2 = jnp.take_along_axis(gates2, ind2[:, None], axis=-1)[:, 0]
            multiplier = jnp.stack([mult1, mult2], axis=-1)
            selected = jnp.stack([ind1, ind2], axis=-1)
            return (multiplier, selected)
        B, S, H = hidden_states.shape
        E = router_w.shape[0]
        x = hidden_states.reshape(-1, H)
        T = x.shape[0]
        logits = x @ router_w.T
        routing_weights, selected = sparsemixer_eval(logits, JITTER_EPS)
        tok = jnp.arange(T)
        dense_w = jnp.zeros((T, E), dtype=x.dtype)
        dense_w = dense_w.at[tok, selected[:, 0]].add(routing_weights[:, 0])
        dense_w = dense_w.at[tok, selected[:, 1]].add(routing_weights[:, 1])
        out = jnp.zeros_like(x)
        for e in range(E):
            h = jax.nn.silu(x @ w_gate[e].T) * (x @ w_up[e].T)
            out = out + dense_w[:, e:e + 1] * (h @ w_down[e].T)
        return out.reshape(B, S, H)
    x = x + _L0_attn_ref(_layernorm(x, axis=-1), L0_attn_latent_w, L0_attn_latent_b, L0_attn_Wd_w, L0_attn_Wd_b, L0_attn_out_w, L0_attn_out_b)
    x = x + _L0_xattn_ref(_layernorm(x, axis=-1), ctx_1024, ctx_1024, L0_xattn_w, L0_xattn_u)
    x = x + _L0_ffn_ref(_layernorm(x, axis=-1), L0_ffn_router_w, L0_ffn_w_gate, L0_ffn_w_up, L0_ffn_w_down)
    return x

_drawn_inputs = setup_inputs


def setup_inputs(seed=0):
    import zlib

    import numpy as np

    out = dict(_drawn_inputs(seed))
    spreads = {}
    factors = {'L0_attn_latent_b': 4.628,
     'L0_attn_Wd_w': 5.832,
     'L0_attn_Wd_b': 64.0,
     'L0_attn_out_b': 2.86,
     'L0_xattn_u': 8.0}
    for name, (base, spread) in spreads.items():
        noise = np.random.default_rng([zlib.crc32(name.encode()), seed]).standard_normal(out[name].shape)
        drawn = base * np.exp(spread * noise) if base else spread * noise
        out[name] = jnp.asarray(drawn.astype(out[name].dtype))
    for name, factor in factors.items():
        out[name] = (out[name] * factor).astype(out[name].dtype)
    return out
```

```python
import numpy as np
import concourse.bass as bass
from concourse import mybir
from contextlib import ExitStack

B, T, C = 16, 128, 256
H, L = 16, 72
NE, F = 8, 512
GB = 4
NG = B // GB
NU = NG * 16
EPS = 1e-5


class Queue:

    def __init__(self, sem):
        self.sem, self.count, self.ops, self.met = sem, 0, [], {}

    def add(self, make, *waits, sig=True):
        need = {}
        for w in waits:
            if w is None:
                continue
            s, v = w
            need[id(s)] = (s, max(v, need.get(id(s), (s, 0))[1]))
        for s, v in need.values():
            if self.met.get(id(s), 0) < v:
                self.met[id(s)] = v
                self.ops.append(("wait", s, v))
        if sig:
            self.count += 1
        self.ops.append(("do", make, self.sem if sig else None))
        return (self.sem, self.count)

    def dma(self, make, sem, total, *waits):
        self.add(make, *waits, sig=False)
        self.ops[-1] = ("dma", make, sem)
        return (sem, total)

    def play(self, eng):
        for kind, a, b in self.ops:
            if kind == "wait":
                eng.wait_ge(a, b)
            elif kind == "dma":
                a(eng).then_inc(b, 16)
            else:
                i = a(eng)
                if b is not None:
                    i.then_inc(b, 1)


def build(nc, x, ctxin, lw, lb, wd, wdb, ow, ob, xw, xu, rw, wf, out):
    fp32 = mybir.dt.float32
    f32r = mybir.dt.float32r
    i32 = mybir.dt.int32
    ALU = mybir.AluOpType
    ACT = mybir.ActivationFunctionType
    AX = mybir.AxisListType

    ctx = ExitStack()
    with ctx:
        def sb(name, shape, dt=fp32, stack=ctx):
            return stack.enter_context(nc.sbuf_tensor(name, shape, dt))

        def sem(name):
            return ctx.enter_context(nc.semaphore(name))

        PE, DVE, SC, PL = (Queue(sem(n)) for n in ("s_pe", "s_dve", "s_act", "s_pool"))
        SP = Queue(sem("s_sp"))

        X = sb("X", [128, B, C])
        XN = sb("XN", [128, GB, C])
        EX = sb("EX", [128, GB, C])
        WKn = sb("WKn", [128, GB, C])
        WKd = sb("WKd", [128, GB, C])
        arena = sb("arena", [128, 3072])
        D0 = sb("D0", [128, 2, 517])
        ident = sb("ident", [128, 128])
        small = sb("small", [128, 1100])
        rwr = sb("rwr", [128, 2, 2, NE], f32r)
        LG = sb("LG", [128, B, NE])
        DW = sb("DW", [128, B, NE])
        with ExitStack() as s0:
            raw = sb("raw", [L, H * C], fp32, s0)
        with ExitStack() as s0:
            sb("pad24", [128, 6144], fp32, s0)
            cxa = sb("cxa", [128, 2048], fp32, s0)
        CX = cxa[:, 0:1024].rearrange("p (b c) -> p b c", b=GB)
        XT2 = [sb(f"XT2_{g}", [128, 2, 2, 512], f32r) for g in range(NG)]
        s1 = ExitStack()
        xnT = sb("xnT", [128, 2, 2, 512], f32r, s1)
        KT = [sb(f"KT{i}", [L, 2, 512], f32r, s1) for i in range(2)]
        V = [sb(f"V{i}", [128, 2, GB, L], f32r, s1) for i in range(2)]
        Vf = sb("Vf", [128, GB, L], fp32, s1)
        qT = [sb(f"qT{i}", [L, 2, 4, 512], f32r, s1) for i in range(2)]
        Wd = sb("Wd", [128, 2, 2, H, L], f32r, s1)
        Ow = sb("Ow", [L, 2, H, C], f32r, s1)
        Lw = sb("Lw", [128, 2, 2, L], f32r, s1)
        obr = sb("obr", [1, 2, C], f32r, s1)
        onr = sb("onr", [1, 128], f32r, s1)
        EB = [sb(f"EB{i}", [128, 4, 128], fp32, s1) for i in range(2)]
        PT = sb("PT", [128, 2, 512], f32r, s1)
        ZT = sb("ZT", [L, 2, 512], f32r, s1)
        maskr = sb("maskr", [128, 4, 128], f32r, s1)
        identr = sb("identr", [128, 128], f32r, s1)
        s1.close()
        WF = [sb(f"WF{i}", [128, 2, 3072], f32r) for i in range(2)]
        SG = [sb(f"SG{i}", [128, 512]) for i in range(2)]
        HF = [sb(f"HF{i}", [128, 512]) for i in range(2)]
        HR = [sb(f"HR{i}", [128, 2, 512], f32r) for i in range(2)]

        P = [ctx.enter_context(nc.psum_tensor(f"P{i}", [128, 512], fp32)) for i in range(6)]
        PO = ctx.enter_context(nc.psum_tensor("PO", [128, 2, 512], fp32))
        QB, SB, PTB, YB, TR = P[0], [P[1], P[2]], P[3], P[4], P[5]

        off = [0]

        def piece(n):
            off[0] += n
            return small[:, off[0] - n:off[0]]

        mv1 = piece(32).rearrange("p (b s) -> p b s", s=2)
        st = piece(24).rearrange("p (b s) -> p b s", s=6)
        rs1 = piece(16)
        ve = piece(16)
        tt = piece(16)
        mv2 = piece(8).rearrange("p (b s) -> p b s", s=2)
        rs2 = piece(4)
        nr = piece(4)
        mr = piece(4)
        NM = [piece(4) for _ in range(2)]
        SM = [piece(4) for _ in range(2)]
        lbc = piece(1)
        lbb = piece(L)
        wdb_s = piece(H)
        xws = piece(2)
        xus = piece(2)
        ew = piece(2)
        rwf = piece(16)
        rt = piece(14 * 32).rearrange("p (n b e) -> p n b e", n=14, e=NE)
        io = piece(32).rearrange("p (b e) -> p b e", e=NE)
        pos = piece(8)
        obf = piece(256)
        assert off[0] <= 1100

        s_x = [sem(f"s_x{g}") for g in range(NG)]
        s_c = sem("s_c")
        s_w = [sem(f"s_w{i}") for i in range(6)]
        s_f = sem("s_f")
        s_out = sem("s_out")
        xv = x.rearrange("b t c -> t b c")
        cv = ctxin.rearrange("b t c -> t b c")
        x_in = []
        rWd = arena[:, 0:2304].rearrange("p (k h l) -> p k h l", k=2, h=H)
        rOw = raw[:, :].rearrange("p (h c) -> p h c", h=H)
        rLw = arena[:, 2304:2304 + 2 * L].rearrange("p (k l) -> p k l", k=2)

        def load_x(g):
            x_in.append(SP.dma(lambda e: e.dma_start(X[:, GB * g:GB * g + GB, :], xv[:, GB * g:GB * g + GB, :]), s_x[g], 16))

        load_x(0)
        n_small = 0
        for dst, src in ((lbc[0:L, :], lb.rearrange("(l a) -> l a", a=1)),
                         (lbb, lb.rearrange("(a l) -> a l", a=1).broadcast_to([128, L])),
                         (wdb_s[0:L, :], wdb), (xws, xw), (xus, xu), (rwf, rw),
                         (obf[0:1, :], ob.rearrange("(a c) -> a c", a=1)), (rLw, lw)):
            n_small += 16
            small_in = SP.dma(lambda e, d=dst, s=src: e.dma_start(d, s), s_w[0], n_small)
        small_in = (s_w[0], n_small)
        wd_in = SP.dma(lambda e: e.dma_start(rWd, wd), s_w[1], 16)
        ctx_in = [SP.dma(lambda e: e.dma_start(CX, cv[:, 0:GB, :]), s_c, 16)]
        for g in range(1, NG):
            load_x(g)
        ow_in = SP.dma(lambda e: e.dma_start(rOw, ow), s_w[2], 16)

        t = PL.add(lambda e: e.memset(ident[:, :], 0.0))
        ident_ok = PL.add(lambda e: e.affine_select(out=ident[:, :], in_=ident[:, :], compare_op=ALU.not_equal, fill=1.0,
                                                    base=0, pattern=[[-1, 128]], channel_multiplier=1), t)
        mf = EX[:, 0:2, :].rearrange("p a (b s) -> p (a b) s", s=128)
        t = PL.add(lambda e: e.memset(mf, 0.0))
        mask_f = PL.add(lambda e: e.affine_select(out=mf, in_=mf, compare_op=ALU.is_ge, fill=-float(2.0 ** 100),
                                                  base=0, pattern=[[0, 4], [-1, 128]], channel_multiplier=1), t)
        iota_ok = PL.add(lambda e: e.iota(io.bitcast(i32), pattern=[[0, GB], [1, NE]], base=0, channel_multiplier=0))
        on_f = PL.add(lambda e: e.memset(XN[0:1, 0, 0:128], 1.0))

        def rsqrt(v, y, n, *waits):
            t = DVE.add(lambda e: e.tensor_scalar(y.bitcast(i32), v.bitcast(i32), -0.5, 1597463007.0, ALU.mult, ALU.add), *waits)
            for _ in range(3):
                t = DVE.add(lambda e: e.tensor_tensor(tt[:, 0:n], y, y, ALU.mult), t)
                t = DVE.add(lambda e: e.scalar_tensor_tensor(out=tt[:, 0:n], in0=tt[:, 0:n], scalar=-0.5, in1=v, op0=ALU.mult, op1=ALU.mult), t)
                t = DVE.add(lambda e: e.scalar_tensor_tensor(out=y, in0=tt[:, 0:n], scalar=1.5, in1=y, op0=ALU.add, op1=ALU.mult), t)
            return t

        def stats(b0, mv, y, *waits):
            ts = [DVE.add(lambda e, b=b: e.bn_stats(st[:, b, :], X[:, b0 + b, :]), *waits) for b in range(GB)]
            for b in range(GB):
                t = DVE.add(lambda e, b=b: e.bn_aggr(mv[:, b, :], st[:, b, :]), ts[b])
            t = DVE.add(lambda e: e.tensor_scalar(ve[:, 0:GB], mv[:, :, 1], EPS, None, ALU.add), t)
            return rsqrt(ve[:, 0:GB], y, GB, t)

        def split(hi, lo, src, *waits):
            a = SC.add(lambda e: e.activation(hi, src, ACT.Copy), *waits)
            return a, DVE.add(lambda e: e.tensor_tensor(lo, src, hi.bitcast(fp32), ALU.subtract), a)

        def split_bias(hi, lo, src, bias, *waits):
            a = SC.add(lambda e: e.activation(hi, src, ACT.Identity, bias=bias), *waits)
            return a, DVE.add(lambda e: e.scalar_tensor_tensor(out=lo, in0=src, scalar=bias, in1=hi.bitcast(fp32),
                                                               op0=ALU.add, op1=ALU.subtract), a)

        def mm3(o, lt, rt_, start, stop, *waits, skip=False):
            for n, (a, b) in enumerate(((0, 0), (0, 1), (1, 0))):
                r = PE.add(lambda e, a=a, b=b, s=start and n == 0, z=stop and n == 2:
                           e.matmul(o, lt(a), rt_(b), start=s, stop=z, skip_group_check=skip),
                           *(waits if n == 0 else ()), sig=stop and n == 2)
            return r

        state = {"tr": [None, None], "xn": None}

        def tr_free():
            return state["tr"]

        lw_ok = split(Lw[:, 0], Lw[:, 1], rLw, small_in)
        rw_ok = split(rwr[:, 0], rwr[:, 1], rwf.rearrange("p (k e) -> p k e", k=2), small_in)
        idr_ok = SC.add(lambda e: e.activation(identr[:, :], ident[:, :], ACT.Copy), ident_ok)
        mask_ok = SC.add(lambda e: e.activation(maskr[:, :, :], mf, ACT.Copy), mask_f)
        on_ok = SC.add(lambda e: e.activation(onr[:, :], XN[0:1, 0, 0:128], ACT.Copy), on_f)
        ob_ok = split(obr[:, 0, :], obr[:, 1, :], obf[0:1, :], small_in)
        ew_ok = SC.add(lambda e: e.activation(ew, xws, ACT.Exp), small_in)
        wdb_ok = DVE.add(lambda e: e.tensor_scalar(wdb_s[0:L, :], wdb_s[0:L, :], 0.25, None, ALU.mult), small_in)

        def d0_fill():
            d = []
            for k in range(2):
                d.append(PL.add(lambda e, k=k: e.tensor_scalar(D0[:, k, :], arena[:, 0:517], ew[:, k:k + 1], None, ALU.add), ew_ok, zero_ok))
            t = None
            for k in range(2):
                t = PL.add(lambda e, k=k: e.memset(D0[:, k, 0:517:129], 0.0), d[k])
            return t

        ln1 = {}
        last_q = {}
        kv = {}

        def ln1_stats(g):
            t = stats(GB * g, mv1[:, GB * g:GB * g + GB, :], rs1[:, GB * g:GB * g + GB], x_in[g])
            ln1[g] = t

        def transposed(dst, w_free):
            done = []
            for k in range(2):
                for b in range(GB):
                    p = PE.add(lambda e, b=b, k=k: e.transpose(TR[:, 128 * b:128 * b + 128], XN[:, b, 128 * k:128 * k + 128], ident[:, :]),
                               state["xn"], ident_ok, *tr_free(), sig=b == GB - 1)
                r = split(dst[:, 0, k, :], dst[:, 1, k, :], TR[:, :], p, w_free)
                state["tr"] = list(r)
                done += r
            state["xn_free"] = p
            return done

        state["xn_free"] = on_ok

        def normalise(b0, mv, y, *waits):
            for b in range(GB):
                t = PL.add(lambda e, b=b: e.tensor_scalar(XN[:, b, :], X[:, b0 + b, :], mv[:, b, 0:1], y[:, b:b + 1],
                                                          ALU.subtract, ALU.mult), state["xn_free"], *waits)
            state["xn"] = t

        def stage_a(g):
            normalise(GB * g, mv1[:, GB * g:GB * g + GB, :], rs1[:, GB * g:GB * g + GB], ln1[g])
            xt = transposed(xnT, last_q.get(g - 1))
            i = g % 2
            old = kv_free.get(g - 2, ())
            for k in range(2):
                p = mm3(QB[0:L, :], lambda a, k=k: Lw[:, a, k, :], lambda a, k=k: xnT[:, a, k, :], k == 0, k == 1,
                        *xt, *lw_ok, *state.get("qb", ()))
            kt = split_bias(KT[i][:, 0, :], KT[i][:, 1, :], QB[0:L, :], lbc[0:L, :], p, *old)
            state["qb"] = kt
            for b in range(GB):
                for k in range(2):
                    p = mm3(TR[:, L * b:L * b + L], lambda a, k=k, b=b: xnT[:, a, k, 128 * b:128 * b + 128],
                            lambda a, k=k: Lw[:, a, k, :], k == 0, k == 1, *tr_free())
            bb = lbb.unsqueeze(1).broadcast_to([128, GB, L])
            t = DVE.add(lambda e: e.tensor_tensor(Vf[:, :, :], TR[:, 0:GB * L].rearrange("p (b l) -> p b l", b=GB), bb, ALU.add),
                        p, small_in, state.get("vf_free"))
            state["tr"] = [t, None]
            v = split(V[i][:, 0], V[i][:, 1], Vf[:, :, :], t, *old)
            state["vf_free"] = v[1]
            kv[g] = (kt, v)

        kv_free = {}

        q_ok = {}
        s_read = {}

        def q_head(hg, j):
            g, h, i = hg // 4, 4 * (hg % 4) + j, hg % 2
            for k in range(2):
                p = mm3(QB[0:L, :], lambda a, k=k: Wd[:, a, k, h, :], lambda a, k=k: xnT[:, a, k, :], k == 0, k == 1,
                        *(wd_ok if k == 0 else ()), *state["qb"])
            last_q[g] = p
            r = split_bias(qT[i][:, 0, j, :], qT[i][:, 1, j, :], QB[0:L, :], wdb_s[0:L, h:h + 1], p, wdb_ok, s_read.get(4 * (hg - 2) + 3))
            state["qb"] = r
            q_ok.setdefault(hg, []).extend(r)

        ep, ev, FA, FB, FC = (arena[:, 518 * i:518 * i + 517] for i in range(5))
        cu, cw = cxa[:, 1024:1536], cxa[:, 1536:2048]
        epv = ep[:, 0:516].rearrange("p (b j) -> p b j", j=129)[:, :, 1:129]
        evv = ev[:, 0:516].rearrange("p (b j) -> p b j", j=129)[:, :, 1:129]
        cuv, cwv = (a[:, 0:512].rearrange("p (b j) -> p b j", j=128) for a in (cu, cw))
        wk_free = {"n": None, "d": None}
        wk_ok = {}
        ar = {"f": (), "s": None}

        def fwd(a):
            return a[:, 0:516].rearrange("p (b j) -> p b j", j=129)[:, :, 0:128]

        def bwd(a):
            return a[:, 1:517].rearrange("p (b j) -> p b j", j=129)[:, :, 1:129]

        def stage_w(g, k):
            cin = ctx_in[g]
            tv = TR[:, :].rearrange("p (b j) -> p b j", j=128)
            for b in range(GB):
                p = PE.add(lambda e, b=b: e.transpose(TR[:, 128 * b:128 * b + 128], CX[:, b, 128 * k:128 * k + 128], ident[:, :]),
                           cin, ident_ok, *tr_free(), sig=b == GB - 1)
            state["cx_free"] = p
            a1 = SC.add(lambda e: e.activation(epv, tv, ACT.Exp), p, zero_ok, *ar["f"])
            a2 = SC.add(lambda e: e.activation(cuv, tv, ACT.Exp, bias=xus[:, k:k + 1]), small_in)
            d1 = DVE.add(lambda e: e.tensor_tensor(evv, tv, epv, ALU.mult), a1, a2)
            d2 = DVE.add(lambda e: e.tensor_tensor(cwv, tv, cuv, ALU.mult), a2)
            state["tr"] = [d2, a2]
            f1 = DVE.add(lambda e: e.tensor_tensor_scan(FA, D0[:, k, :], ep, 0.0, ALU.mult, ALU.add), d0_ok, a1, *ar["f"])
            f2 = DVE.add(lambda e: e.tensor_tensor_scan(FB[:, ::-1], D0[:, k, ::-1], ep[:, ::-1], 0.0, ALU.mult, ALU.add))
            g1 = DVE.add(lambda e: e.tensor_tensor_scan(FC, D0[:, k, :], ev, 0.0, ALU.mult, ALU.add), d1)
            p1 = PL.add(lambda e: e.tensor_tensor(cuv, cuv, fwd(FA), ALU.add), f1, a2, d2)
            p2 = PL.add(lambda e: e.tensor_tensor(cuv, cuv, bwd(FB), ALU.add), f2, p1)
            g2 = DVE.add(lambda e: e.tensor_tensor_scan(FA[:, ::-1], D0[:, k, ::-1], ev[:, ::-1], 0.0, ALU.mult, ALU.add), p1)
            p3 = PL.add(lambda e: e.tensor_tensor(cwv, cwv, fwd(FC), ALU.add), g1, d2)
            p4 = PL.add(lambda e: e.tensor_tensor(cwv, cwv, bwd(FA), ALU.add), g2, p3)
            last = []
            for key, src, dst, ok in (("d", cuv, WKd, p2), ("n", cwv, WKn, p4)):
                for b in range(GB):
                    p = PE.add(lambda e, b=b, src=src: e.transpose(TR[:, 128 * b:128 * b + 128], src[:, b, :], ident[:, :]),
                               ok, *tr_free(), sig=b == GB - 1)
                last.append(p)
                a = SC.add(lambda e, dst=dst: e.activation(dst[:, :, 128 * k:128 * k + 128], tv, ACT.Copy), p, wk_free[key])
                state["tr"] = [a, None]
                wk_ok[key] = a
            ar["f"] = (last[0], last[1], g2, p4)
            state["cx_free"] = last[1]
            if k == 1 and g + 1 < NG:
                ctx_in.append(SP.dma(lambda e: e.dma_start(CX, cv[:, GB * (g + 1):GB * (g + 2), :]), s_c, 16 * (g + 2),
                                     state["cx_free"]))

        exp_ok, p_ok, pt_ok, y_done, z_ok, o_done, t_done = {}, {}, {}, {}, {}, {}, {}

        def unit(n):
            return n // 16, (n % 16) // 4, n % 4

        def stage_s(n):
            g, hq, b = unit(n)
            i, S = (n // 4) % 2, SB[n % 2]
            k = KT[g % 2]
            p = PE.add(lambda e: e.matmul(S[:, :], identr[:, :], maskr[:, :, :].rearrange("p a b -> p (a b)"), start=True, stop=False,
                                          skip_group_check=True), idr_ok, mask_ok, exp_ok.get(n - 2), sig=False)
            for j in range(4):
                p = mm3(S[:, 128 * j:128 * j + 128], lambda a, j=j: qT[i][:, a, j, 128 * b:128 * b + 128],
                        lambda a: k[:, a, 128 * b:128 * b + 128], False, True, *(q_ok[n // 4] + list(kv[g][0]) if j == 0 else ()), skip=True)
            s_read[n] = p
            Sv = S[:, :].rearrange("p (h s) -> p h s", h=4)
            d = DVE.add(lambda e: e.tensor_reduce(NM[n % 2], Sv, AX.X, ALU.max, negate=True), p, exp_ok.get(n - 2))
            for j in range(4):
                a = SC.add(lambda e, j=j: e.activation(EB[n % 2][:, j, :], S[:, 128 * j:128 * j + 128], ACT.Exp, bias=NM[n % 2][:, j:j + 1],
                                                       accum_out=SM[n % 2][:, j:j + 1]), d, t_done.get(n - 2), p_ok.get(n - 2))
            exp_ok[n] = a
            d = DVE.add(lambda e: e.reciprocal(SM[n % 2], SM[n % 2]), a)
            p_ok[n] = PL.add(lambda e: e.tensor_tensor(EB[n % 2][:, :, :], EB[n % 2][:, :, :],
                                                       SM[n % 2].unsqueeze(2).broadcast_to([128, 4, 128]), ALU.mult), d)

        def stage_t(n):
            for j in range(4):
                p = PE.add(lambda e, j=j: e.transpose(PTB[:, 128 * j:128 * j + 128], EB[n % 2][:, j, :], ident[:, :]),
                           p_ok[n], ident_ok, *pt_ok.get(n - 1, ()), sig=j == 3)
            t_done[n] = p
            pt_ok[n] = split(PT[:, 0, :], PT[:, 1, :], PTB[:, :], p, y_done.get(n - 1))

        def stage_y(n):
            g, hq, b = unit(n)
            v = V[g % 2]
            y_done[n] = mm3(YB[0:L, :], lambda a: v[:, a, b, :], lambda a: PT[:, a, :], True, True,
                            *pt_ok[n], *kv[g][1], *z_ok.get(n - 1, ()))
            kv_free[g] = (s_read[n], y_done[n])
            z_ok[n] = split(ZT[:, 0, :], ZT[:, 1, :], YB[0:L, :], y_done[n], o_done.get(n - 1))

        def stage_o(n):
            g, hq, b = unit(n)
            o = PO[:, b // 2, 256 * (b % 2):256 * (b % 2) + 256]
            if hq == 0:
                for a in range(2):
                    PE.add(lambda e, a=a: e.matmul(o, onr[:, :], obr[:, a, :], start=a == 0 and b % 2 == 0, stop=False, skip_group_check=True),
                           on_ok, *ob_ok, state.get("o_free"), sig=False)
            for j in range(4):
                h = 4 * hq + j
                p = mm3(o, lambda a, j=j: ZT[:, a, 128 * j:128 * j + 128], lambda a, h=h: Ow[:, a, h, :], False, j == 3,
                        *z_ok[n], *ow_ok, skip=True)
            o_done[n] = p

        ev_ = {}

        def e_add(g):
            v = X[:, GB * g:GB * g + GB, :]
            t = DVE.add(lambda e: e.tensor_tensor(v, PO[:, :, :].rearrange("p a (b c) -> p (a b) c", b=2), v, ALU.add),
                        o_done[16 * g + 15], state["xn"])
            state["o_free"] = t
            ev_["x1"] = t

        def e_ln2(g):
            t = stats(GB * g, mv2, rs2, ev_["x1"], ev_.get("nr_free"))
            a = DVE.add(lambda e: e.tensor_scalar(nr, rs2, -1.0, None, ALU.mult), t)
            ev_["nr"] = DVE.add(lambda e: e.tensor_tensor(mr, mv2[:, :, 0], rs2, ALU.mult), t)

        def e_sig(g):
            for b in range(GB):
                a = SC.add(lambda e, b=b: e.activation(EX[:, b, :], X[:, GB * g + b, :], ACT.Exp, bias=mr[:, b:b + 1], scale=nr[:, b:b + 1]),
                           ev_["nr"], mask_ok, ev_.get("x2"))
            ev_["nr_free"] = a
            ev_["d"] = DVE.add(lambda e: e.scalar_tensor_tensor(out=EX[:, :, :].rearrange("p b c -> p (b c)"),
                                                                in0=EX[:, :, :].rearrange("p b c -> p (b c)"), scalar=1.0,
                                                                in1=WKd[:, :, :].rearrange("p b c -> p (b c)"), op0=ALU.add, op1=ALU.mult),
                               a, wk_ok["d"])
            wk_free["d"] = ev_["d"]

        def e_rec(g, b):
            r = DVE.add(lambda e: e.reciprocal(EX[:, b, :], EX[:, b, :]), ev_["d"])
            p = PL.add(lambda e: e.tensor_tensor(EX[:, b, :], EX[:, b, :], WKn[:, b, :], ALU.mult), r, wk_ok["n"])
            wk_free["n"] = p
            ev_["x2"] = PL.add(lambda e: e.tensor_tensor(X[:, GB * g + b, :], X[:, GB * g + b, :], EX[:, b, :], ALU.add), p, ev_["nr_free"])

        def e_ln3(g):
            t = stats(GB * g, mv2, rs2, ev_["x2"], ev_["nr_free"])
            normalise(GB * g, mv2, rs2, t)

        xt2_ok = {}

        def e_xt(g):
            free = [wsp for wsp in (ev_.get("raw_free"),) if wsp is not None]
            w = state["cx_free"] if g == NG - 1 else None
            xt2_ok[g] = transposed(XT2[g], w)
            for b in range(GB):
                for k in range(2):
                    p = mm3(TR[:, NE * b:NE * b + NE], lambda a, k=k, b=b: XT2[g][:, a, k, 128 * b:128 * b + 128],
                            lambda a, k=k: rwr[:, a, k, :], k == 0, k == 1, *xt2_ok[g], *rw_ok, *tr_free())
            t = DVE.add(lambda e: e.tensor_copy(LG[:, GB * g:GB * g + GB, :], TR[:, 0:GB * NE].rearrange("p (b e) -> p b e", e=NE)), p)
            state["tr"] = [t, None]
            ev_["lg"] = t

        dw_ok = {}

        def router(g):
            s = LG[:, GB * g:GB * g + GB, :]
            ab, a1, keep, key, oh1, s2, e1, e2, m8, dlt, oh2, k2, red, red2 = (rt[:, i] for i in range(14))

            def bc(a):
                return a.unsqueeze(2).broadcast_to([128, GB, NE])

            m1, i1, z1, m2, i2, z2 = (
                red[:, 0, 0:4], red[:, 1, 0:4], red[:, 2, 0:4], red[:, 3, 0:4], red2[:, 0, 0:4], red2[:, 1, 0:4])
            add = DVE.add

            def tt_(o, p, q, op, *w):
                return add(lambda e: e.tensor_tensor(o, p, q, op), *w)

            def stt(o, p, sc, q, op0, op1, *w):
                return add(lambda e: e.scalar_tensor_tensor(out=o, in0=p, scalar=sc, in1=q, op0=op0, op1=op1), *w)

            n_abs = add(lambda e: e.tensor_scalar(ab, s, -1.0, None, ALU.mult), ev_["lg"], ev_.get("router"))
            n_abs = tt_(ab, ab, s, ALU.max, n_abs)
            t = add(lambda e: e.tensor_reduce(m1, s, AX.X, ALU.max), ev_["lg"])
            ta = tt_(a1, s, bc(m1), ALU.is_lt, t)
            ta = stt(key, a1, float(NE), ios, ALU.mult, ALU.add, ta, ios_ok)
            ta = add(lambda e: e.tensor_reduce(i1, key, AX.X, ALU.min), ta)
            ta = tt_(oh1, ios, bc(i1), ALU.is_equal, ta)
            ts2 = stt(s2, oh1, -3.0e38, s, ALU.mult, ALU.add, ta)

            def gate(m, sc, oh, z, e_, *w):
                f = tt_(a1, ab, bc(m), ALU.max, *w)
                d = tt_(dlt, bc(m), s, ALU.subtract, *w)
                f = stt(keep, a1, 0.02, dlt, ALU.mult, ALU.is_ge, f, d)
                d = tt_(m8, sc, bc(m), ALU.subtract, *w)
                x_ = SC.add(lambda e: e.activation(e_, m8, ACT.Exp), d)
                f = tt_(e_, e_, keep, ALU.mult, x_, f)
                f = add(lambda e: e.tensor_reduce(z, e_, AX.X, ALU.add), f)
                return add(lambda e: e.reciprocal(z, z), f)

            z1_ok = gate(m1, s, oh1, z1, e1, t, n_abs, ta)
            t = add(lambda e: e.tensor_reduce(m2, s2, AX.X, ALU.max), ts2)
            tb = tt_(a1, s2, bc(m2), ALU.is_lt, t, z1_ok)
            tb = stt(key, a1, float(NE), ios, ALU.mult, ALU.add, tb)
            tb = add(lambda e: e.tensor_reduce(i2, key, AX.X, ALU.min), tb)
            tb = tt_(oh2, ios, bc(i2), ALU.is_equal, tb)
            z2_ok = gate(m2, s2, oh2, z2, e2, t, tb)
            c = tt_(oh1, oh1, bc(z1), ALU.mult, z1_ok, ts2)
            d = tt_(oh2, oh2, bc(z2), ALU.mult, z2_ok)
            dw_ok[g] = ev_["router"] = tt_(DW[:, GB * g:GB * g + GB, :], oh1, oh2, ALU.add, c, d)

        ios = piece(32).rearrange("p (b e) -> p b e", e=NE)
        ios_ok = DVE.add(lambda e: e.tensor_copy(ios, io.bitcast(i32)), iota_ok)

        ln1_stats(0)
        wd_ok = [SC.add(lambda e: e.activation(Wd[:, 0], rWd, ACT.Copy, scale=0.25), wd_in)]
        wd_ok.append(DVE.add(lambda e: e.scalar_tensor_tensor(out=Wd[:, 1].rearrange("p k h l -> p (k h l)"),
                                                              in0=rWd.rearrange("p k h l -> p (k h l)"), scalar=0.25,
                                                              in1=Wd[:, 0].bitcast(fp32).rearrange("p k h l -> p (k h l)"),
                                                              op0=ALU.mult, op1=ALU.subtract), wd_ok[0]))
        stage_a(0)
        zero_ok = PL.add(lambda e: e.memset(arena[:, :], 0.0), *wd_ok, *lw_ok)
        d0_ok = d0_fill()
        for j in range(4):
            q_head(0, j)
        ow_ok = list(split(Ow[:, 0], Ow[:, 1], rOw, ow_in))
        raw_done = (wd_ok[0], wd_ok[1], ow_ok[0], ow_ok[1])

        wf_in, wf_ok = {}, {}
        wfv = arena[:, 0:3072]

        def load_wf(e_):
            wf_in[e_] = SP.dma(lambda e: e.dma_start(wfv, wf[e_]), s_f, 16 * (e_ + 1),
                               *(ar["f"] if e_ == 0 else wf_ok[e_ - 1]))

        hooks = {}

        def at(n, f, *a):
            hooks.setdefault(n, []).append((f, a))

        for g in range(NG):
            at(16 * g + 9, stage_w, g, 0)
            at(16 * g + 12, stage_w, g, 1)
            if g:
                at(16 * g - 6, ln1_stats, g)
            s = 16 * (g + 1) + 1
            at(s, e_add, g)
            at(s + 1, e_ln2, g)
            at(s + 2, e_sig, g)
            for b in range(GB):
                at(s + 3 + b // 2, e_rec, g, b)
            at(s + 5, e_ln3, g)
            at(s + 6, e_xt, g)
            at(s + 7, router, g)
        at(16 * NG - 2, load_wf, 0)

        for n in range(NU + 2):
            if n < NU and n % 16 == 12 and n // 16 + 1 < NG:
                stage_a(n // 16 + 1)
            if n < NU:
                stage_s(n)
            if 1 <= n <= NU:
                stage_t(n - 1)
            if n >= 2:
                stage_o(n - 2)
            if n // 4 + 1 < 4 * NG and n < NU:
                q_head(n // 4 + 1, n % 4)
            if 1 <= n <= NU:
                stage_y(n - 1)
            for f, a in hooks.pop(n, ()):
                f(*a)

        att_done = (o_done[NU - 1], (SC.sem, SC.count), (DVE.sem, DVE.count), (PL.sem, PL.count))

        GP, UP = [P[0], P[1]], [P[2], P[3]]

        def split_wf(e_):
            i = e_ % 2
            w = ffn_last.get(e_ - 2)
            ww = (wf_in[e_], w) + (att_done if e_ < 2 else ())
            out_ = []
            for a, b in ((0, 1024), (1024, 2048), (2048, 3072)):
                h = DVE.add(lambda e, a=a, b=b: e.tensor_copy(WF[i][:, 0, a:b], wfv[:, a:b]), *ww)
                out_.append(PL.add(lambda e, a=a, b=b: e.tensor_tensor(WF[i][:, 1, a:b], wfv[:, a:b], WF[i][:, 0, a:b].bitcast(fp32), ALU.subtract), h))
            wf_ok[e_] = (h, out_[-1])
            return out_

        down_done, ffn_last = {}, {}
        wparts = {}
        wparts[0] = split_wf(0)
        units = [(e_, tc, fc) for e_ in range(NE) for tc in range(NG) for fc in range(4)]
        gu_done, g_read, h_ok, hr_free, sg_free, comb = {}, {}, {}, {}, {}, {}
        OBK = [PO, None]
        O2 = [P[4], P[5]]

        def obank(m, t):
            return (PO[:, t // 2, 256 * (t % 2):256 * (t % 2) + 256] if m % 2 == 0 else
                    O2[t // 2][:, 256 * (t % 2):256 * (t % 2) + 256])

        def up_stage(u):
            e_, tc, fc = units[u]
            w = WF[e_ % 2]
            i = u % 2
            gate = w[:, :, 0:1024].rearrange("p a (k f) -> p a k f", k=2)
            up = w[:, :, 1024:2048].rearrange("p a (k f) -> p a k f", k=2)
            extra = att_done if u < 4 else ()
            for k in range(2):
                p1 = mm3(GP[i][:, :], lambda a, k=k: gate[:, a, k, 128 * fc:128 * fc + 128], lambda a, k=k: XT2[tc][:, a, k, :],
                         k == 0, k == 1, wparts[e_][0], *xt2_ok[tc], *g_read.get(u - 2, ()), *extra)
            for k in range(2):
                p2 = mm3(UP[i][:, :], lambda a, k=k: up[:, a, k, 128 * fc:128 * fc + 128], lambda a, k=k: XT2[tc][:, a, k, :],
                         k == 0, k == 1, wparts[e_][1])
            a = SC.add(lambda e: e.activation(SG[i][:, :], GP[i][:, :], ACT.Silu), p1, *g_read.get(u - 2, ()), *extra)
            d = DVE.add(lambda e: e.tensor_tensor(HF[i][:, :], SG[i][:, :], UP[i][:, :], ALU.mult), a, p2, *h_ok.get(u - 2, ()), *extra)
            g_read[u] = (a, d)
            hi = SC.add(lambda e: e.activation(HR[i][:, 0, :], HF[i][:, :], ACT.Copy), d, hr_free.get(u - 2))
            lo = PL.add(lambda e: e.tensor_tensor(HR[i][:, 1, :], HF[i][:, :], HR[i][:, 0, :].bitcast(fp32), ALU.subtract), hi)
            h_ok[u] = (hi, lo)

        def down_stage(u):
            e_, tc, fc = units[u]
            m, i = u // 4, u % 2
            dn = WF[e_ % 2][:, :, 2048:3072].rearrange("p a (f d) -> p a f d", f=4)
            for t in range(GB):
                p = mm3(obank(m, t), lambda a, t=t: HR[i][:, a, 128 * t:128 * t + 128], lambda a: dn[:, a, fc, :],
                        fc == 0 and t % 2 == 0, fc == 3 or t == 3, *h_ok[u], wparts[e_][2], *(comb.get(m - 2, ())),
                        *((state["tr"][0], state["tr"][1], state["o_free"]) if m < 2 else ()), skip=True)
            hr_free[u] = p
            if fc == 3:
                ts = []
                for t in range(GB):
                    b = GB * tc + t
                    ts.append(DVE.add(lambda e, t=t, b=b: e.scalar_tensor_tensor(out=X[:, b, :], in0=obank(m, t), scalar=DW[:, b, e_:e_ + 1],
                                                                            in1=X[:, b, :], op0=ALU.mult, op1=ALU.add),
                                      p, dw_ok[tc], ev_["x2"], *comb.get(m - NG, ())))
                comb[m] = tuple(ts)
                if tc == NG - 1:
                    ffn_last[e_] = p
                if e_ == NE - 1:
                    ov = out.rearrange("b t c -> t b c")
                    SP.dma(lambda e: e.dma_start(ov[:, GB * tc:GB * tc + GB, :], X[:, GB * tc:GB * tc + GB, :]), s_out, 16 * (tc + 1), *ts)

        for u in range(len(units)):
            for f, a in hooks.pop(NU + 2 + u, ()):
                f(*a)
            e_, tc, fc = units[u]
            if tc == 0 and fc == 1 and e_ + 1 < NE:
                load_wf(e_ + 1)
            if tc == 1 and fc == 1 and e_ + 1 < NE:
                wparts[e_ + 1] = split_wf(e_ + 1)
            up_stage(u)
            if u:
                down_stage(u - 1)
        down_stage(len(units) - 1)
        SP.ops.append(("wait", s_out, 16 * NG))
        assert not hooks

        block = ctx.enter_context(nc.Block())

        @block.sync
        def _(eng):
            SP.play(eng)

        @block.tensor
        def _(eng):
            PE.play(eng)

        @block.vector
        def _(eng):
            DVE.play(eng)

        @block.scalar
        def _(eng):
            SC.play(eng)

        @block.gpsimd
        def _(eng):
            PL.play(eng)


def _lay(inputs):
    g = {k: np.asarray(v) for k, v in inputs.items()}
    wg = g["L0_ffn_w_gate"].transpose(0, 2, 1).reshape(NE, 2, 128, F).transpose(0, 2, 1, 3).reshape(NE, 128, 2 * F)
    wu = g["L0_ffn_w_up"].transpose(0, 2, 1).reshape(NE, 2, 128, F).transpose(0, 2, 1, 3).reshape(NE, 128, 2 * F)
    wn = g["L0_ffn_w_down"].transpose(0, 2, 1).reshape(NE, 4, 128, C).transpose(0, 2, 1, 3).reshape(NE, 128, 4 * C)
    a = {
        "x": g["x"], "ctxin": g["ctx_1024"],
        "lw": g["L0_attn_latent_w"].reshape(2, 128, L).transpose(1, 0, 2),
        "lb": g["L0_attn_latent_b"],
        "wd": g["L0_attn_Wd_w"].reshape(H, 2, 128, L).transpose(2, 1, 0, 3),
        "wdb": g["L0_attn_Wd_b"].T,
        "ow": g["L0_attn_out_w"].reshape(H, L, C).transpose(1, 0, 2),
        "ob": g["L0_attn_out_b"],
        "xw": g["L0_xattn_w"].reshape(2, 128).T,
        "xu": g["L0_xattn_u"].reshape(2, 128).T,
        "rw": g["L0_ffn_router_w"].T.reshape(2, 128, NE).transpose(1, 0, 2).reshape(128, 2 * NE),
        "wf": np.concatenate([wg, wu, wn], axis=2),
    }
    return {k: np.ascontiguousarray(v) for k, v in a.items()}


def kernel(**inputs):
    import concourse.bacc as bacc
    from concourse.bass_utils import run_bass_kernel_spmd as run

    nc = bacc.Bacc("TRN2", target_bir_lowering=False, num_devices=1)
    arrays = _lay(inputs)
    args = {n: nc.dram_tensor(n, a.shape, mybir.dt.from_np(a.dtype), kind="ExternalInput").ap() for n, a in arrays.items()}
    out = nc.dram_tensor("out", (B, T, C), mybir.dt.float32, kind="ExternalOutput").ap()
    build(nc, **args, out=out)
    r = run(nc, [arrays], core_ids=[0])
    return r.results[0]["out"]
```

```python
import numpy as np
import concourse.bass as bass
from concourse import mybir
from contextlib import ExitStack

B, T, C = 16, 128, 256
H, L = 16, 72
NE, F = 8, 512
GB = 4
NG = B // GB
NU = NG * 16
EPS = 1e-5
TN = B * T
TW = 256
CAP = TN + TW
NT = (2 * TN + NE * (TW - 1)) // TW
RW = C + 2
NX = 5
NOWHERE = 1 << 20


class Queue:

    def __init__(self, sem):
        self.sem, self.count, self.ops, self.met = sem, 0, [], {}

    def add(self, make, *waits, sig=True):
        need = {}
        for w in waits:
            if w is None:
                continue
            s, v = w
            need[id(s)] = (s, max(v, need.get(id(s), (s, 0))[1]))
        for s, v in need.values():
            if self.met.get(id(s), 0) < v:
                self.met[id(s)] = v
                self.ops.append(("wait", s, v))
        if sig:
            self.count += 1
        self.ops.append(("do", make, self.sem if sig else None))
        return (self.sem, self.count)

    def dma(self, make, sem, total, *waits):
        self.add(make, *waits, sig=False)
        self.ops[-1] = ("dma", make, sem)
        return (sem, total)

    def play(self, eng):
        for kind, a, b in self.ops:
            if kind == "wait":
                eng.wait_ge(a, b)
            elif kind == "dma":
                a(eng).then_inc(b, 16)
            else:
                i = a(eng)
                if b is not None:
                    i.then_inc(b, 1)


def build(nc, x, ctxin, lw, lb, wd, wdb, ow, ob, xw, xu, rw, wf, out, xs):
    fp32 = mybir.dt.float32
    f32r = mybir.dt.float32r
    i32 = mybir.dt.int32
    ALU = mybir.AluOpType
    ACT = mybir.ActivationFunctionType
    AX = mybir.AxisListType

    ctx = ExitStack()
    with ctx:
        def sb(name, shape, dt=fp32, stack=ctx):
            return stack.enter_context(nc.sbuf_tensor(name, shape, dt))

        def sem(name):
            return ctx.enter_context(nc.semaphore(name))

        PE, DVE, SC, PL = (Queue(sem(n)) for n in ("s_pe", "s_dve", "s_act", "s_pool"))
        SP = Queue(sem("s_sp"))

        X = sb("X", [128, B, C])
        XN = sb("XN", [128, GB, RW])
        EX = sb("EX", [128, GB, C])
        WKn = sb("WKn", [128, GB, C])
        WKd = sb("WKd", [128, GB, C])
        arena = sb("arena", [128, 3072])
        D0 = sb("D0", [128, 2, 517])
        ident = sb("ident", [128, 128])
        small = sb("small", [128, 1794])
        rwr = sb("rwr", [128, 2, 2, NE], f32r)
        LG = sb("LG", [128, GB, NE])
        xnTb = sb("xnTb", [128, 2, 2, 512], f32r)
        Utr = sb("Utr", [128, 128], f32r)
        onem = sb("onem", [128, 128], f32r)
        Mr = sb("Mr", [128, GB, NE], f32r)
        SL = sb("SL", [128, NG, 2, GB], i32)
        PI = sb("PI", [1, NE + 2 * NT], i32)
        with ExitStack() as s0:
            raw = sb("raw", [L, H * C], fp32, s0)
        cxa = sb("cxa", [128, 2048])
        CX = cxa[:, 0:1024].rearrange("p (b c) -> p b c", b=GB)
        XT3 = sb("XT3", [128, 2, 2, 512], f32r)
        s1 = ExitStack()
        xnTa = sb("xnTa", [128, 2, 2, 512], f32r, s1)
        Wd = sb("Wd", [128, 2, 2, H, L], f32r, s1)
        KT = [sb(f"KT{i}", [L, 2, 512], f32r, s1) for i in range(2)]
        V = [sb(f"V{i}", [128, 2, GB, L], f32r, s1) for i in range(2)]
        Vf = sb("Vf", [128, GB, L], fp32, s1)
        qT = [sb(f"qT{i}", [L, 2, 4, 512], f32r, s1) for i in range(2)]
        Ow = sb("Ow", [L, 2, H, C], f32r, s1)
        Lw = sb("Lw", [128, 2, 2, L], f32r, s1)
        obr = sb("obr", [1, 2, C], f32r, s1)
        onr = sb("onr", [1, 128], f32r, s1)
        EB = [sb(f"EB{i}", [128, 4, 128], fp32, s1) for i in range(2)]
        PT = sb("PT", [128, 2, 512], f32r, s1)
        ZT = sb("ZT", [L, 2, 512], f32r, s1)
        maskr = sb("maskr", [128, 4, 128], f32r, s1)
        identr = sb("identr", [128, 128], f32r, s1)
        s1.close()
        xnTs = [xnTa, xnTb]
        WF = [sb(f"WF{i}", [128, 2, 3072], f32r) for i in range(2)]
        WR = [sb(f"WR{i}", [128, 3072]) for i in range(2)]
        XG = [sb(f"XG{i}", [128, 2, RW]) for i in range(NX)]
        GT = [sb(f"GT{i}", [128, 2, 2, TW], f32r) for i in range(2)]
        SG = [sb(f"SG{i}", [128, 512]) for i in range(2)]
        HF = [sb(f"HF{i}", [128, 512]) for i in range(2)]
        HR = [sb(f"HR{i}", [128, 2, 4, TW], f32r) for i in range(2)]
        Y = [sb(f"Y{i}", [128, 2, C]) for i in range(2)]
        ZF = sb("ZF", [128, 2, RW])

        P = [ctx.enter_context(nc.psum_tensor(f"P{i}", [128, 512], fp32)) for i in range(6)]
        PO = ctx.enter_context(nc.psum_tensor("PO", [128, 2, 512], fp32))
        QB, SB, PTB, YB, TR = P[0], [P[1], P[2]], P[3], P[4], P[5]

        off = [0]

        def piece(n):
            off[0] += n
            return small[:, off[0] - n:off[0]]

        mv1 = piece(32).rearrange("p (b s) -> p b s", s=2)
        st = piece(24).rearrange("p (b s) -> p b s", s=6)
        rs1 = piece(16)
        ve = piece(16)
        tt = piece(16)
        mv2 = piece(8).rearrange("p (b s) -> p b s", s=2)
        rs2 = piece(4)
        nr = piece(4)
        mr = piece(4)
        NM = [piece(4) for _ in range(2)]
        SM = [piece(4) for _ in range(2)]
        lbc = piece(1)
        lbb = piece(L)
        wdb_s = piece(H)
        xws = piece(2)
        xus = piece(2)
        ew = piece(2)
        rwf = piece(16)
        rt = piece(14 * 32).rearrange("p (n b e) -> p n b e", n=14, e=NE)
        io = piece(32).rearrange("p (b e) -> p b e", e=NE)
        pos = piece(8)
        obf = piece(256)
        RUN = piece(5 * NE).rearrange("p (b e) -> p b e", e=NE)
        ecap = piece(NE)
        tok = piece(B)
        jio = piece(NT)
        big = piece(NT * NE).rearrange("p (j e) -> p j e", e=NE)
        big2 = piece(NT * NE).rearrange("p (j e) -> p j e", e=NE)
        pl = piece(16 * NE).rearrange("p (n e) -> p n e", e=NE)
        pj = piece(8 * NT).rearrange("p (n j) -> p n j", j=NT)
        assert off[0] <= 1794

        s_x = [sem(f"s_x{g}") for g in range(NG)]
        s_c = sem("s_c")
        s_w = [sem(f"s_w{i}") for i in range(6)]
        s_sc = sem("s_sc")
        s_fill = sem("s_fill")
        s_wf = [[sem(f"s_wf{i}_{k}") for k in range(3)] for i in range(2)]
        s_xg = [sem(f"s_xg{i}") for i in range(NX)]
        s_add = sem("s_add")
        s_out = sem("s_out")
        xv = x.rearrange("b t c -> t b c")
        cv = ctxin.rearrange("b t c -> t b c")
        x_in = []
        rWd = arena[:, 0:2304].rearrange("p (k h l) -> p k h l", k=2, h=H)
        rOw = raw[:, :].rearrange("p (h c) -> p h c", h=H)
        rLw = arena[:, 2304:2304 + 2 * L].rearrange("p (k l) -> p k l", k=2)

        def load_x(g):
            x_in.append(SP.dma(lambda e: e.dma_start(X[:, GB * g:GB * g + GB, :], xv[:, GB * g:GB * g + GB, :]), s_x[g], 16))

        load_x(0)
        n_small = 0
        for dst, src in ((lbc[0:L, :], lb.rearrange("(l a) -> l a", a=1)),
                         (lbb, lb.rearrange("(a l) -> a l", a=1).broadcast_to([128, L])),
                         (wdb_s[0:L, :], wdb), (xws, xw), (xus, xu), (rwf, rw),
                         (obf[0:1, :], ob.rearrange("(a c) -> a c", a=1)), (rLw, lw)):
            n_small += 16
            small_in = SP.dma(lambda e, d=dst, s=src: e.dma_start(d, s), s_w[0], n_small)
        small_in = (s_w[0], n_small)
        wd_in = SP.dma(lambda e: e.dma_start(rWd, wd), s_w[1], 16)
        ow_in = SP.dma(lambda e: e.dma_start(rOw, ow), s_w[2], 16)
        for g in range(1, NG):
            load_x(g)

        t = PL.add(lambda e: e.memset(ident[:, :], 0.0))
        ident_ok = PL.add(lambda e: e.affine_select(out=ident[:, :], in_=ident[:, :], compare_op=ALU.not_equal, fill=1.0,
                                                    base=0, pattern=[[-1, 128]], channel_multiplier=1), t)
        mf = EX[:, 0:2, :].rearrange("p a (b s) -> p (a b) s", s=128)
        t = PL.add(lambda e: e.memset(mf, 0.0))
        mask_f = PL.add(lambda e: e.affine_select(out=mf, in_=mf, compare_op=ALU.is_ge, fill=-float(2.0 ** 100),
                                                  base=0, pattern=[[0, 4], [-1, 128]], channel_multiplier=1), t)
        iota_ok = PL.add(lambda e: e.iota(io.bitcast(i32), pattern=[[0, GB], [1, NE]], base=0, channel_multiplier=0))
        ut_f = EX[:, 2, 0:128]
        t = PL.add(lambda e: e.memset(ut_f, 1.0))
        ut_ok = PL.add(lambda e: e.affine_select(out=ut_f, in_=ut_f, compare_op=ALU.is_gt, fill=0.0, base=0,
                                                 pattern=[[1, 128]], channel_multiplier=-1), t)
        on_f = PL.add(lambda e: e.memset(XN[:, 0, 0:128], 1.0))
        PL.add(lambda e: e.iota(tok.bitcast(i32), pattern=[[T, B]], base=0, channel_multiplier=1))
        PL.add(lambda e: e.iota(pl[:, 0, :].bitcast(i32), pattern=[[CAP, NE]], base=0, channel_multiplier=0))
        idx_ok = PL.add(lambda e: e.iota(pj[:, 0, :].bitcast(i32), pattern=[[1, NT]], base=0, channel_multiplier=0))

        def rsqrt(v, y, n, *waits):
            t = DVE.add(lambda e: e.tensor_scalar(y.bitcast(i32), v.bitcast(i32), -0.5, 1597463007.0, ALU.mult, ALU.add), *waits)
            for _ in range(3):
                yield
                t = DVE.add(lambda e: e.tensor_tensor(tt[:, 0:n], y, y, ALU.mult), t)
                t = DVE.add(lambda e: e.scalar_tensor_tensor(out=tt[:, 0:n], in0=tt[:, 0:n], scalar=-0.5, in1=v, op0=ALU.mult, op1=ALU.mult), t)
                t = DVE.add(lambda e: e.scalar_tensor_tensor(out=y, in0=tt[:, 0:n], scalar=1.5, in1=y, op0=ALU.add, op1=ALU.mult), t)
            return t

        def stats(b0, mv, y, *waits):
            ts = [DVE.add(lambda e, b=b: e.bn_stats(st[:, b, :], X[:, b0 + b, :]), *waits) for b in range(2)]
            yield
            ts += [DVE.add(lambda e, b=b: e.bn_stats(st[:, b, :], X[:, b0 + b, :]), *waits) for b in range(2, 4)]
            yield
            for b in range(GB):
                t = DVE.add(lambda e, b=b: e.bn_aggr(mv[:, b, :], st[:, b, :]), ts[b])
            t = DVE.add(lambda e: e.tensor_scalar(ve[:, 0:GB], mv[:, :, 1], EPS, None, ALU.add), t)
            return (yield from rsqrt(ve[:, 0:GB], y, GB, t))

        def split(hi, lo, src, *waits):
            a = SC.add(lambda e: e.activation(hi, src, ACT.Copy), *waits)
            return a, DVE.add(lambda e: e.tensor_tensor(lo, src, hi.bitcast(fp32), ALU.subtract), a)

        def split_bias(hi, lo, src, bias, *waits):
            a = SC.add(lambda e: e.activation(hi, src, ACT.Identity, bias=bias), *waits)
            return a, DVE.add(lambda e: e.scalar_tensor_tensor(out=lo, in0=src, scalar=bias, in1=hi.bitcast(fp32),
                                                               op0=ALU.add, op1=ALU.subtract), a)

        def mm3(o, lt, rt_, start, stop, *waits, skip=False):
            for n, (a, b) in enumerate(((0, 0), (0, 1), (1, 0))):
                r = PE.add(lambda e, a=a, b=b, s=start and n == 0, z=stop and n == 2:
                           e.matmul(o, lt(a), rt_(b), start=s, stop=z, skip_group_check=skip),
                           *(waits if n == 0 else ()), sig=stop and n == 2)
            return r

        state = {"tr": [None, None], "xn": None}

        def tr_free():
            return state["tr"]

        lw_ok = split(Lw[:, 0], Lw[:, 1], rLw, small_in)
        rw_ok = split(rwr[:, 0], rwr[:, 1], rwf.rearrange("p (k e) -> p k e", k=2), small_in)
        idr_ok = SC.add(lambda e: e.activation(identr[:, :], ident[:, :], ACT.Copy), ident_ok)
        mask_ok = SC.add(lambda e: e.activation(maskr[:, :, :], mf, ACT.Copy), mask_f)
        utr_ok = SC.add(lambda e: e.activation(Utr[:, :], ut_f, ACT.Copy), ut_ok)
        onem_ok = SC.add(lambda e: e.activation(onem[:, :], XN[:, 0, 0:128], ACT.Copy), on_f)
        on_ok = SC.add(lambda e: e.activation(onr[:, :], XN[0:1, 0, 0:128], ACT.Copy), on_f)
        ob_ok = split(obr[:, 0, :], obr[:, 1, :], obf[0:1, :], small_in)
        ew_ok = SC.add(lambda e: e.activation(ew, xws, ACT.Exp), small_in)
        wdb_ok = DVE.add(lambda e: e.tensor_scalar(wdb_s[0:L, :], wdb_s[0:L, :], 0.25, None, ALU.mult), small_in)

        def d0_fill():
            d = []
            for k in range(2):
                d.append(PL.add(lambda e, k=k: e.tensor_scalar(D0[:, k, :], arena[:, 0:517], ew[:, k:k + 1], None, ALU.add), ew_ok, zero_ok))
            t = None
            for k in range(2):
                t = PL.add(lambda e, k=k: e.memset(D0[:, k, 0:517:129], 0.0), d[k])
            return t

        ln1 = {}
        last_q = {}
        kv = {}

        def ln1_stats(g):
            ln1[g] = yield from stats(GB * g, mv1[:, GB * g:GB * g + GB, :], rs1[:, GB * g:GB * g + GB], x_in[g])

        def transposed(dst, w_free, *more):
            done = []
            for k in range(2):
                for b in range(GB):
                    p = PE.add(lambda e, b=b, k=k: e.transpose(TR[:, 128 * b:128 * b + 128], XN[:, b, 128 * k:128 * k + 128], ident[:, :]),
                               state["xn"], ident_ok, *tr_free(), sig=b == GB - 1)
                r = split(dst[:, 0, k, :], dst[:, 1, k, :], TR[:, :], p, w_free, *more)
                state["tr"] = list(r)
                done += r
                yield
            state["xn_free"] = p
            return done

        state["xn_free"] = on_ok

        def normalise(b0, mv, y, *waits):
            for b in range(GB):
                t = DVE.add(lambda e, b=b: e.tensor_scalar(XN[:, b, 0:C], X[:, b0 + b, :], mv[:, b, 0:1], y[:, b:b + 1],
                                                           ALU.subtract, ALU.mult), state["xn_free"], *waits)
                if b == 1:
                    yield
            state["xn"] = t

        def stage_a(g):
            yield from normalise(GB * g, mv1[:, GB * g:GB * g + GB, :], rs1[:, GB * g:GB * g + GB], ln1[g])
            yield
            xnT = xnTs[g % 2]
            xt = yield from transposed(xnT, last_q.get(g - 2))
            xt_ok[g] = xt
            i = g % 2
            old = kv_free.get(g - 2, ())
            for k in range(2):
                p = mm3(QB[0:L, :], lambda a, k=k: Lw[:, a, k, :], lambda a, k=k: xnT[:, a, k, :], k == 0, k == 1,
                        *xt, *lw_ok, *state.get("qb", ()))
            kt = split_bias(KT[i][:, 0, :], KT[i][:, 1, :], QB[0:L, :], lbc[0:L, :], p, *old)
            state["qb"] = kt
            yield
            for b in range(GB):
                if b == 2:
                    yield
                for k in range(2):
                    p = mm3(TR[:, L * b:L * b + L], lambda a, k=k, b=b: xnT[:, a, k, 128 * b:128 * b + 128],
                            lambda a, k=k: Lw[:, a, k, :], k == 0, k == 1, *tr_free())
            yield
            bb = lbb.unsqueeze(1).broadcast_to([128, GB, L])
            t = DVE.add(lambda e: e.tensor_tensor(Vf[:, :, :], TR[:, 0:GB * L].rearrange("p (b l) -> p b l", b=GB), bb, ALU.add),
                        p, small_in, state.get("vf_free"))
            state["tr"] = [t, None]
            v = split(V[i][:, 0], V[i][:, 1], Vf[:, :, :], t, *old)
            state["vf_free"] = v[1]
            kv[g] = (kt, v)

        kv_free = {}
        xt_ok = {}

        q_ok = {}
        s_read = {}

        def q_head(hg, j, bank=None):
            g, h, i = hg // 4, 4 * (hg % 4) + j, hg % 2
            xnT = xnTs[g % 2]
            Q, q_free = (QB, state["qb"]) if bank is None else (bank, state["q" + bank.name])
            for k in range(2):
                p = mm3(Q[0:L, :], lambda a, k=k: Wd[:, a, k, h, :], lambda a, k=k: xnT[:, a, k, :], k == 0, k == 1,
                        *(wd_ok + xt_ok[g] if k == 0 else ()), *q_free)
            last_q[g] = p
            r = split_bias(qT[i][:, 0, j, :], qT[i][:, 1, j, :], Q[0:L, :], wdb_s[0:L, h:h + 1], p, wdb_ok, s_read.get(4 * (hg - 2) + 3))
            state["qb" if bank is None else "q" + bank.name] = r
            q_ok.setdefault(hg, []).extend(r)

        ep, ev, FA, FB, FC = (arena[:, 518 * i:518 * i + 517] for i in range(5))
        cu, cw = cxa[:, 1024:1536], cxa[:, 1536:2048]
        epv = ep[:, 0:516].rearrange("p (b j) -> p b j", j=129)[:, :, 1:129]
        evv = ev[:, 0:516].rearrange("p (b j) -> p b j", j=129)[:, :, 1:129]
        cuv, cwv = (a[:, 0:512].rearrange("p (b j) -> p b j", j=128) for a in (cu, cw))
        wk_free = {"n": None, "d": None}
        wk_ok = {}
        ar = {"f": (), "s": None}

        def fwd(a):
            return a[:, 0:516].rearrange("p (b j) -> p b j", j=129)[:, :, 0:128]

        def bwd(a):
            return a[:, 1:517].rearrange("p (b j) -> p b j", j=129)[:, :, 1:129]

        def stage_w(g, k):
            cin = ctx_in[g]
            tv = TR[:, :].rearrange("p (b j) -> p b j", j=128)
            for b in range(GB):
                p = PE.add(lambda e, b=b: e.transpose(TR[:, 128 * b:128 * b + 128], CX[:, b, 128 * k:128 * k + 128], ident[:, :]),
                           cin, ident_ok, *tr_free(), sig=b == GB - 1)
            yield
            a1 = SC.add(lambda e: e.activation(epv, tv, ACT.Exp), p, zero_ok, *ar["f"])
            a2 = SC.add(lambda e: e.activation(cuv, tv, ACT.Exp, bias=xus[:, k:k + 1]), small_in)
            d1 = DVE.add(lambda e: e.tensor_tensor(evv, tv, epv, ALU.mult), a1, a2)
            d2 = DVE.add(lambda e: e.tensor_tensor(cwv, tv, cuv, ALU.mult), a2)
            state["tr"] = [d2, a2]
            yield
            f1 = DVE.add(lambda e: e.tensor_tensor_scan(FA, D0[:, k, :], ep, 0.0, ALU.mult, ALU.add), d0_ok, a1, *ar["f"])
            f2 = DVE.add(lambda e: e.tensor_tensor_scan(FB[:, ::-1], D0[:, k, ::-1], ep[:, ::-1], 0.0, ALU.mult, ALU.add))
            yield
            g1 = DVE.add(lambda e: e.tensor_tensor_scan(FC, D0[:, k, :], ev, 0.0, ALU.mult, ALU.add), d1)
            p1 = PL.add(lambda e: e.tensor_tensor(cuv, cuv, fwd(FA), ALU.add), f1, a2, d2)
            p2 = PL.add(lambda e: e.tensor_tensor(cuv, cuv, bwd(FB), ALU.add), f2, p1)
            g2 = DVE.add(lambda e: e.tensor_tensor_scan(FA[:, ::-1], D0[:, k, ::-1], ev[:, ::-1], 0.0, ALU.mult, ALU.add), p1)
            yield
            p3 = PL.add(lambda e: e.tensor_tensor(cwv, cwv, fwd(FC), ALU.add), g1, d2)
            p4 = PL.add(lambda e: e.tensor_tensor(cwv, cwv, bwd(FA), ALU.add), g2, p3)
            yield
            last = []
            for key, src, dst, ok in (("d", cuv, WKd, p2), ("n", cwv, WKn, p4)):
                for b in range(GB):
                    p = PE.add(lambda e, b=b, src=src: e.transpose(TR[:, 128 * b:128 * b + 128], src[:, b, :], ident[:, :]),
                               ok, *tr_free(), sig=b == GB - 1)
                last.append(p)
                a = SC.add(lambda e, dst=dst: e.activation(dst[:, :, 128 * k:128 * k + 128], tv, ACT.Copy), p, wk_free[key])
                state["tr"] = [a, None]
                wk_ok[key] = a
                yield
            ar["f"] = (last[0], last[1], g2, p4)
            state["cx_free"] = last[1]
            if k == 1 and g + 1 < NG:
                ctx_in.append(SP.dma(lambda e: e.dma_start(CX, cv[:, GB * (g + 1):GB * (g + 2), :]), s_c, 16 * (g + 2),
                                     state["cx_free"]))

        exp_ok, p_ok, pt_ok, y_done, z_ok, o_done, t_done = {}, {}, {}, {}, {}, {}, {}

        def unit(n):
            return n // 16, (n % 16) // 4, n % 4

        def stage_s(n):
            g, hq, b = unit(n)
            i, S = (n // 4) % 2, SB[n % 2]
            k = KT[g % 2]
            p = PE.add(lambda e: e.matmul(S[:, :], identr[:, :], maskr[:, :, :].rearrange("p a b -> p (a b)"), start=True, stop=False,
                                          skip_group_check=True), idr_ok, mask_ok, exp_ok.get(n - 2), sig=False)
            for j in range(4):
                p = mm3(S[:, 128 * j:128 * j + 128], lambda a, j=j: qT[i][:, a, j, 128 * b:128 * b + 128],
                        lambda a: k[:, a, 128 * b:128 * b + 128], False, True, *(q_ok[n // 4] + list(kv[g][0]) if j == 0 else ()), skip=True)
            s_read[n] = p
            Sv = S[:, :].rearrange("p (h s) -> p h s", h=4)
            d = DVE.add(lambda e: e.tensor_reduce(NM[n % 2], Sv, AX.X, ALU.max, negate=True), p, exp_ok.get(n - 2))
            for j in range(4):
                a = SC.add(lambda e, j=j: e.activation(EB[n % 2][:, j, :], S[:, 128 * j:128 * j + 128], ACT.Exp, bias=NM[n % 2][:, j:j + 1],
                                                       accum_out=SM[n % 2][:, j:j + 1]), d, t_done.get(n - 2), p_ok.get(n - 2))
            exp_ok[n] = a

        def stage_n(n):
            d = DVE.add(lambda e: e.reciprocal(SM[n % 2], SM[n % 2]), exp_ok[n])
            p_ok[n] = PL.add(lambda e: e.tensor_tensor(EB[n % 2][:, :, :], EB[n % 2][:, :, :],
                                                       SM[n % 2].unsqueeze(2).broadcast_to([128, 4, 128]), ALU.mult), d)

        def stage_t(n):
            for j in range(4):
                p = PE.add(lambda e, j=j: e.transpose(PTB[:, 128 * j:128 * j + 128], EB[n % 2][:, j, :], ident[:, :]),
                           p_ok[n], ident_ok, *pt_ok.get(n - 1, ()), sig=j == 3)
            t_done[n] = p
            pt_ok[n] = split(PT[:, 0, :], PT[:, 1, :], PTB[:, :], p, y_done.get(n - 1))

        def stage_y(n):
            g, hq, b = unit(n)
            v = V[g % 2]
            y_done[n] = mm3(YB[0:L, :], lambda a: v[:, a, b, :], lambda a: PT[:, a, :], True, True,
                            *pt_ok[n], *kv[g][1], *z_ok.get(n - 1, z_first))
            kv_free[g] = (s_read[n], y_done[n])
            z_ok[n] = split(ZT[:, 0, :], ZT[:, 1, :], YB[0:L, :], y_done[n], o_done.get(n - 1))

        def stage_o(n):
            g, hq, b = unit(n)
            o = PO[:, b // 2, 256 * (b % 2):256 * (b % 2) + 256]
            if hq == 0:
                for a in range(2):
                    PE.add(lambda e, a=a: e.matmul(o, onr[:, :], obr[:, a, :], start=a == 0 and b % 2 == 0, stop=False, skip_group_check=True),
                           on_ok, *ob_ok, state.get("o_free"), sig=False)
            for j in range(4):
                h = 4 * hq + j
                p = mm3(o, lambda a, j=j: ZT[:, a, 128 * j:128 * j + 128], lambda a, h=h: Ow[:, a, h, :], False, j == 3,
                        *z_ok[n], *ow_ok[hq], skip=True)
            o_done[n] = p

        ev_ = {}

        def e_add(g):
            v = X[:, GB * g:GB * g + GB, :]
            t = DVE.add(lambda e: e.tensor_tensor(v, PO[:, :, :].rearrange("p a (b c) -> p (a b) c", b=2), v, ALU.add),
                        o_done[16 * g + 15], state["xn"])
            state["o_free"] = t
            ev_["x1"] = t

        def e_ln2(g):
            t = yield from stats(GB * g, mv2, rs2, ev_["x1"], ev_.get("nr_free"))
            a = DVE.add(lambda e: e.tensor_scalar(nr, rs2, -1.0, None, ALU.mult), t)
            ev_["nr"] = DVE.add(lambda e: e.tensor_tensor(mr, mv2[:, :, 0], rs2, ALU.mult), t)

        def e_sig(g):
            for b in range(GB):
                a = SC.add(lambda e, b=b: e.activation(EX[:, b, :], X[:, GB * g + b, :], ACT.Exp, bias=mr[:, b:b + 1], scale=nr[:, b:b + 1]),
                           ev_["nr"], mask_ok, utr_ok, ev_.get("x2"))
                if b == 1:
                    yield
            ev_["nr_free"] = a
            ev_["d"] = DVE.add(lambda e: e.scalar_tensor_tensor(out=EX[:, :, :].rearrange("p b c -> p (b c)"),
                                                                in0=EX[:, :, :].rearrange("p b c -> p (b c)"), scalar=1.0,
                                                                in1=WKd[:, :, :].rearrange("p b c -> p (b c)"), op0=ALU.add, op1=ALU.mult),
                               a, wk_ok["d"])
            wk_free["d"] = ev_["d"]

        def e_rec(g, b):
            r = DVE.add(lambda e: e.reciprocal(EX[:, b, :], EX[:, b, :]), ev_["d"])
            p = PL.add(lambda e: e.tensor_tensor(EX[:, b, :], EX[:, b, :], WKn[:, b, :], ALU.mult), r, wk_ok["n"])
            wk_free["n"] = p
            ev_["x2"] = PL.add(lambda e: e.tensor_tensor(X[:, GB * g + b, :], X[:, GB * g + b, :], EX[:, b, :], ALU.add), p, ev_["nr_free"])

        def e_ln3(g):
            t = yield from stats(GB * g, mv2, rs2, ev_["x2"], ev_["nr_free"])
            yield from normalise(GB * g, mv2, rs2, t)


        def e_xt(g):
            yield
            xt3 = yield from transposed(XT3, ev_.get("xt3_free"), *ow_ok[3])
            yield
            for b in range(GB):
                for k in range(2):
                    p = mm3(TR[:, NE * b:NE * b + NE], lambda a, k=k, b=b: XT3[:, a, k, 128 * b:128 * b + 128],
                            lambda a, k=k: rwr[:, a, k, :], k == 0, k == 1, *xt3, *rw_ok, *tr_free())
            ev_["xt3_free"] = p
            t = DVE.add(lambda e: e.tensor_copy(LG[:, :, :], TR[:, 0:GB * NE].rearrange("p (b e) -> p b e", e=NE)), p, ev_.get("router"))
            state["tr"] = [t, None]
            ev_["lg"] = t

        dw_ok = {}

        def router(g):
            s = LG[:, :, :]
            ab, a1, keep, key, oh1, s2, e1, e2, m8, dlt, oh2, k2, red, red2 = (rt[:, i] for i in range(14))

            def bc(a):
                return a.unsqueeze(2).broadcast_to([128, GB, NE])

            m1, i1, z1, m2, i2, z2 = (
                red[:, 0, 0:4], red[:, 1, 0:4], red[:, 2, 0:4], red[:, 3, 0:4], red2[:, 0, 0:4], red2[:, 1, 0:4])
            add = DVE.add

            def tt_(o, p, q, op, *w):
                return add(lambda e: e.tensor_tensor(o, p, q, op), *w)

            def stt(o, p, sc, q, op0, op1, *w):
                return add(lambda e: e.scalar_tensor_tensor(out=o, in0=p, scalar=sc, in1=q, op0=op0, op1=op1), *w)

            n_abs = add(lambda e: e.tensor_scalar(ab, s, -1.0, None, ALU.mult), ev_["lg"], ev_.get("router"))
            n_abs = tt_(ab, ab, s, ALU.max, n_abs)
            t = add(lambda e: e.tensor_reduce(m1, s, AX.X, ALU.max), ev_["lg"])
            yield
            ta = tt_(a1, s, bc(m1), ALU.is_lt, t)
            ta = stt(key, a1, float(NE), ios, ALU.mult, ALU.add, ta, ios_ok)
            ta = add(lambda e: e.tensor_reduce(i1, key, AX.X, ALU.min), ta)
            ta = tt_(oh1, ios, bc(i1), ALU.is_equal, ta)
            ts2 = stt(s2, oh1, -3.0e38, s, ALU.mult, ALU.add, ta)

            def gate(m, sc, oh, z, e_, *w):
                f = tt_(a1, ab, bc(m), ALU.max, *w)
                d = tt_(dlt, bc(m), s, ALU.subtract, *w)
                f = stt(keep, a1, 0.02, dlt, ALU.mult, ALU.is_ge, f, d)
                yield
                d = tt_(m8, sc, bc(m), ALU.subtract, *w)
                x_ = SC.add(lambda e: e.activation(e_, m8, ACT.Exp), d)
                yield
                f = tt_(e_, e_, keep, ALU.mult, x_, f)
                f = add(lambda e: e.tensor_reduce(z, e_, AX.X, ALU.add), f)
                return add(lambda e: e.reciprocal(z, z), f)

            yield
            z1_ok = yield from gate(m1, s, oh1, z1, e1, t, n_abs, ta)
            yield
            t = add(lambda e: e.tensor_reduce(m2, s2, AX.X, ALU.max), ts2)
            tb = tt_(a1, s2, bc(m2), ALU.is_lt, t, z1_ok)
            tb = stt(key, a1, float(NE), ios, ALU.mult, ALU.add, tb)
            tb = add(lambda e: e.tensor_reduce(i2, key, AX.X, ALU.min), tb)
            tb = tt_(oh2, ios, bc(i2), ALU.is_equal, tb)
            yield
            z2_ok = yield from gate(m2, s2, oh2, z2, e2, t, tb)
            yield
            yield
            m = tt_(Mr[:, :, :], oh1, oh2, ALU.add, tb, ta, ev_.get("m_free"))
            PE.add(lambda e: e.matmul(TR[:, 0:32], Utr[:, :], Mr[:, :, :].rearrange("p b e -> p (b e)"), start=True, stop=True),
                   m, utr_ok, *tr_free(), sig=False)
            p = PE.add(lambda e: e.matmul(TR[:, 32:64], onem[:, :], Mr[:, :, :].rearrange("p b e -> p (b e)"), start=True, stop=True),
                       onem_ok)
            ev_["m_free"] = p
            before = TR[:, 0:32].rearrange("p (b e) -> p b e", e=NE)
            count = TR[:, 32:64].rearrange("p (b e) -> p b e", e=NE)
            yield
            t = add(lambda e: e.tensor_copy(RUN[:, 0, :], RUN[:, 4, :]), ev_["run"], p)
            for b in range(GB):
                t = tt_(RUN[:, b + 1, :], RUN[:, b, :], count[:, b, :], ALU.add, t)
            ev_["run"] = t
            yield
            t = tt_(key, before, RUN[:, 0:4, :], ALU.add, t)
            state["tr"] = [t, None]
            c = tt_(a1, oh1, key, ALU.mult, t, z2_ok)
            c = add(lambda e: e.tensor_reduce(m1, a1, AX.X, ALU.add), c)
            c = add(lambda e: e.tensor_copy(SL[:, g, 0, :], m1), c)
            yield
            d = tt_(a1, oh2, key, ALU.mult, c)
            d = add(lambda e: e.tensor_reduce(m1, a1, AX.X, ALU.add), d)
            d = add(lambda e: e.tensor_copy(SL[:, g, 1, :], m1), d)
            k1 = add(lambda e: e.tensor_copy(XN[:, :, C:C + 1].rearrange("p b a -> p (b a)").bitcast(i32), tok[:, GB * g:GB * g + GB].bitcast(i32)),
                     idx_ok, state["xn"])
            k2_ = add(lambda e: e.tensor_copy(XN[:, :, C + 1:C + 2].rearrange("p b a -> p (b a)"), z1), state["xn"])
            yield
            yield from scatter(g, 0, c, k1, k2_)
            for _ in range(6 if g < NG - 1 else 0):
                yield
            k2_ = add(lambda e: e.tensor_copy(XN[:, :, C + 1:C + 2].rearrange("p b a -> p (b a)"), z2), (s_sc, sc_n[0]))
            ev_["router"] = k2_
            yield
            yield from scatter(g, 1, d, k2_)
            state["xn_free"] = (s_sc, sc_n[0])

        sc_n = [0]

        def scatter(g, side_, *waits):
            for b in range(GB):
                sc_n[0] += 16
                PL.dma(lambda e, b=b: e.indirect_dma_start(xs, bass.IndirectOffsetOnAxis(ap=SL[:, g, side_, b:b + 1], axis=0), XN[:, b, :], None),
                       s_sc, sc_n[0], *waits)
                if b % 2:
                    yield

        def plan():
            add = DVE.add
            nf, tl, te, one = (pl[0:1, i, :] for i in range(1, 5))
            fj, eid, base, rs, un, tmp = (pj[0:1, i, :] for i in range(6))
            add(lambda e: e.tensor_copy(PI[0:1, 0:NE], RUN[0:1, 4, :]), ev_["run"])
            add(lambda e: e.memset(one, 1.0))
            t = add(lambda e: e.scalar_tensor_tensor(out=nf, in0=RUN[0:1, 4, :], scalar=float(TW - 1), in1=ecap[0:1, :], op0=ALU.add, op1=ALU.subtract))
            t = add(lambda e: e.tensor_copy(tl.bitcast(i32), nf), t)
            t = add(lambda e: e.tensor_scalar(tl.bitcast(i32), tl.bitcast(i32), 8, None, ALU.logical_shift_right), t)
            t = add(lambda e: e.tensor_copy(nf, tl.bitcast(i32)), t)
            te_ok = add(lambda e: e.tensor_tensor_scan(te, one, nf, 0.0, ALU.mult, ALU.add), t)
            tb = te.unsqueeze(1).broadcast_to([1, NT, NE])
            jb = jio[0:1, :].unsqueeze(2).broadcast_to([1, NT, NE])
            ge_ok = add(lambda e: e.tensor_tensor(big[0:1], tb, jb, ALU.is_le), te_ok)
            t1 = add(lambda e: e.tensor_reduce(eid, big[0:1], AX.X, ALU.add), ge_ok)
            t2 = add(lambda e: e.tensor_tensor(big2[0:1], big[0:1], tb, ALU.mult), ge_ok)
            t3 = add(lambda e: e.tensor_reduce(base, big2[0:1], AX.X, ALU.max), t2)
            t4 = add(lambda e: e.tensor_scalar(un, eid, float(NE), None, ALU.is_ge), t1)
            t5 = add(lambda e: e.tensor_scalar(eid, eid, float(NE - 1), None, ALU.min), t4)
            ie = add(lambda e: e.tensor_copy(PI[0:1, NE:NE + NT], eid), t5)
            t6 = add(lambda e: e.tensor_tensor(tmp, jio[0:1, :], base, ALU.subtract), t3)
            t6 = add(lambda e: e.tensor_scalar(tmp, tmp, float(TW), None, ALU.mult), t6)
            t6 = add(lambda e: e.scalar_tensor_tensor(out=rs, in0=eid, scalar=float(CAP), in1=tmp, op0=ALU.mult, op1=ALU.add), t6)
            t7 = add(lambda e: e.tensor_scalar(tmp, rs, -1.0, RUN[0:1, 4, NE - 1:NE], ALU.mult, ALU.add), t6)
            t7 = add(lambda e: e.tensor_tensor(tmp, tmp, un, ALU.mult), t7)
            t7 = add(lambda e: e.tensor_tensor(rs, rs, tmp, ALU.add), t7)
            return ie, add(lambda e: e.tensor_copy(PI[0:1, NE + NT:NE + 2 * NT], rs), t7)

        ios = piece(32).rearrange("p (b e) -> p b e", e=NE)
        ios_ok = DVE.add(lambda e: e.tensor_copy(ios, io.bitcast(i32)), iota_ok)
        DVE.add(lambda e: e.tensor_copy(ecap, pl[:, 0, :].bitcast(i32)), idx_ok)
        DVE.add(lambda e: e.tensor_copy(jio, pj[:, 0, :].bitcast(i32)), idx_ok)
        ev_["run"] = DVE.add(lambda e: e.tensor_copy(RUN[:, 4, :], pl[:, 0, :].bitcast(i32)), idx_ok)

        ctx_in = []
        def run_all(it):
            for _ in it:
                pass

        run_all(ln1_stats(0))
        wd_ok = [SC.add(lambda e: e.activation(Wd[:, 0], rWd, ACT.Copy, scale=0.25), wd_in)]
        wd_ok.append(DVE.add(lambda e: e.scalar_tensor_tensor(out=Wd[:, 1].rearrange("p k h l -> p (k h l)"),
                                                              in0=rWd.rearrange("p k h l -> p (k h l)"), scalar=0.25,
                                                              in1=Wd[:, 0].bitcast(fp32).rearrange("p k h l -> p (k h l)"),
                                                              op0=ALU.mult, op1=ALU.subtract), wd_ok[0]))
        run_all(stage_a(0))
        zero_ok = PL.add(lambda e: e.memset(arena[:, :], 0.0), *wd_ok, *lw_ok)
        d0_ok = d0_fill()
        for j in range(4):
            state["q" + YB.name] = state.get("q" + YB.name, ())
            q_head(0, j, YB if j % 2 else None)
        ow_ok, z_first = [], state["q" + YB.name]

        def split_ow():
            for h in range(0, H, 4):
                ow_ok.append(split(Ow[:, 0, h:h + 4, :], Ow[:, 1, h:h + 4, :], rOw[:, h:h + 4, :], ow_in))
                yield

        def side(g):
            if g == 0:
                yield from split_ow()
                ctx_in.append(SP.dma(lambda e: e.dma_start(CX, cv[:, 0:GB, :]), s_c, 16, *[t for pair in ow_ok for t in pair]))
            if g + 1 < NG:
                yield from ln1_stats(g + 1)
                yield from stage_a(g + 1)
                yield
            if g:
                yield from e_second(g - 1)
            if g < NG:
                yield from stage_w(g, 0)
                yield from stage_w(g, 1)
            if g:
                yield from e_third(g - 1)

        def e_second(g):
            yield from e_ln2(g)
            yield
            yield from e_sig(g)
            yield
            for b in range(GB):
                e_rec(g, b)
                yield

        ov = out.rearrange("b t c -> t b c")
        out_ok = []

        def e_third(g):
            out_ok.append(SP.dma(lambda e: e.dma_start(ov[:, GB * g:GB * g + GB, :], X[:, GB * g:GB * g + GB, :]), s_out, 16 * (g + 1), ev_["x2"]))
            yield from e_ln3(g)
            yield from e_xt(g)
            yield
            yield from router(g)


        work = iter(())
        used = []

        def turn(k=1):
            for _ in range(k):
                if next(work, 0) == 0:
                    return
                used[-1] += 1

        for n in range(NU + 3):
            state["step"] = n
            if n in (0, 19, 35, 51):
                assert next(work, 0) == 0, "side work is left over"
                work = side(n // 16)
                used.append(0)
            if 2 <= n < NU + 2:
                stage_t(n - 2)
            if n < NU:
                stage_s(n)
            turn()
            if n >= 3:
                stage_o(n - 3)
            turn(2)
            if n < NU:
                stage_n(n)
            if n // 4 + 1 < 4 * NG and n < NU:
                q_head(n // 4 + 1, n % 4)
            turn(1)
            if 2 <= n < NU + 2:
                stage_y(n - 2)
            turn()
            if n >= 18 and (n - 2) % 16 == 0:
                e_add((n - 2) // 16 - 1)

        att_done = (o_done[NU - 1], (SC.sem, SC.count), (DVE.sem, DVE.count), (PL.sem, PL.count))

        assert next(work, 0) == 0
        for _ in side(NG):
            pass
        e_ok, r_ok = plan()

        GP, UP, TG = [P[0], P[1]], [P[2], P[3]], P[4]
        outr = out.rearrange("b t c -> (b t) c")
        fill_f = PL.add(lambda e: e.memset(ZF[:, :, :], 0.0), *att_done)
        fill_ok = PL.add(lambda e: e.memset(ZF[:, :, C:C + 1].bitcast(i32), NOWHERE), fill_f)
        parts = ((0, 1024), (1024, 2048), (2048, 3072))
        w_in, w_ok, w_free, raw_free = {}, {}, {}, {}
        xg_in, gt_ok, gt_free, xg_free = {}, {}, {}, {}
        g_read, h_ok, h_free, o_read, y_ok, up_done = {}, {}, {}, {}, {}, {}

        def load_w(j, k):
            i, (a, b) = j % 2, parts[k]
            if j >= NT:
                return

            def make(e):
                v = e.value_load(PI[0:1, NE + j:NE + j + 1], min_val=0, max_val=NE - 1)
                return e.dma_start(WR[i][:, a:b], wf[bass.ds(v, 1), :, a:b].rearrange("a p n -> (a p) n"))

            w_in[j, k] = SP.dma(make, s_wf[i][k], 16 * (j // 2 + 1), e_ok, *att_done, *raw_free.get((j - 2, k), ()))

        def load_xg(j):
            i = j % NX

            def make(e):
                v = e.value_load(PI[0:1, NE + NT + j:NE + NT + j + 1], min_val=0, max_val=NE * CAP - TW)
                return e.dma_start(XG[i][:, :, :], xs[bass.ds(v, TW), :].rearrange("(a p) c -> p a c", p=128))

            xg_in[j] = SP.dma(make, s_xg[i], 16 * (j // NX + 1), r_ok, (s_sc, sc_n[0]), (s_fill, 16 * NE), *att_done, *xg_free.get(j - NX, ()))

        def fill(k):
            def make(e):
                v = e.value_load(PI[0:1, k:k + 1], min_val=k * CAP, max_val=k * CAP + TN)
                return e.dma_start(xs[bass.ds(v, TW), :].rearrange("(p a) c -> p a c", a=2), ZF[:, :, :])

            SP.dma(make, s_fill, 16 * (k + 1), e_ok, fill_ok)

        def split_w(j, k):
            i, (a, b) = j % 2, parts[k]
            if j >= NT:
                return
            h = SC.add(lambda e: e.activation(WF[i][:, 0, a:b], WR[i][:, a:b], ACT.Copy), w_in[j, k],
                       (w_free if k == 2 else up_done).get(j - 2))
            t = DVE.add(lambda e: e.tensor_tensor(WF[i][:, 1, a:b], WR[i][:, a:b], WF[i][:, 0, a:b].bitcast(fp32), ALU.subtract), h)
            w_ok[j, k] = raw_free[j, k] = (h, t)
            load_w(j + 2, k)

        def turn_x(j):
            for k in range(2):
                for a in range(2):
                    p = PE.add(lambda e, k=k, a=a: e.transpose(TG[:, 256 * k + 128 * a:256 * k + 128 * a + 128],
                                                               XG[j % NX][:, a, 128 * k:128 * k + 128], ident[:, :]),
                               xg_in[j], *gt_ok.get(j - 1, ()), sig=k + a == 2)
            o = GT[j % 2]
            gt_ok[j] = split(o[:, 0, :, :], o[:, 1, :, :], TG[:, :].rearrange("p (k t) -> p k t", k=2), p, up_done.get(j - 2))

        def up_half(j, n):
            w, x_ = WF[j % 2], GT[j % 2]
            gate = w[:, :, 0:1024].rearrange("p a (k f) -> p a k f", k=2)
            up = w[:, :, 1024:2048].rearrange("p a (k f) -> p a k f", k=2)
            u = 2 * j + n
            res = []
            for bank, m, k0 in ((GP[n], gate, 0), (UP[n], up, 1)):
                for q in range(2):
                    fc = 2 * n + q
                    for k in range(2):
                        p = mm3(bank[:, TW * q:TW * q + TW], lambda a, k=k, fc=fc, m=m: m[:, a, k, 128 * fc:128 * fc + 128],
                                lambda a, k=k: x_[:, a, k, :], k == 0, k == 1, *w_ok[j, k0], *gt_ok[j], *g_read.get(u - 2, ()))
                res.append(p)
            up_done[j] = p
            i = n
            a = SC.add(lambda e: e.activation(SG[i][:, :], GP[n][:, :], ACT.Silu), res[0], *g_read.get(u - 2, ()))
            d = DVE.add(lambda e: e.tensor_tensor(HF[i][:, :], SG[i][:, :], UP[n][:, :], ALU.mult), a, res[1], *h_ok.get(u - 2, ()))
            g_read[u] = (a, d)

        def split_h(j, n):
            r = HR[j % 2][:, :, 2 * n:2 * n + 2, :]
            h_ok[2 * j + n] = split(r[:, 0], r[:, 1], HF[n][:, :].rearrange("p (f t) -> p f t", f=2), g_read[2 * j + n][1], h_free.get(j - 2))

        def down(j):
            dn = WF[j % 2][:, :, 2048:3072].rearrange("p a (f d) -> p a f d", f=4)
            O = PO[:, j % 2, :]
            for a_ in range(2):
                for fc in range(4):
                    p = mm3(O[:, C * a_:C * a_ + C], lambda a, fc=fc, a_=a_: HR[j % 2][:, a, fc, 128 * a_:128 * a_ + 128], lambda a, fc=fc: dn[:, a, fc, :],
                            fc == 0, fc == 3, *w_ok[j, 2], *h_ok[2 * j], *h_ok[2 * j + 1], o_read.get(j - 2))
            h_free[j] = w_free[j] = p
            for a_ in range(2):
                t = SC.add(lambda e, a_=a_: e.activation(Y[j % 2][:, a_, :], O[:, C * a_:C * a_ + C], ACT.Copy, scale=XG[j % NX][:, a_, C + 1:C + 2]),
                           p, (s_add, 32 * (j - 1)) if j > 1 else None)
            o_read[j] = t
            for a_ in range(2):
                PL.dma(lambda e, a_=a_: e.indirect_dma_start(outr, bass.IndirectOffsetOnAxis(ap=XG[j % NX][:, a_, C:C + 1].bitcast(i32), axis=0),
                                                             Y[j % 2][:, a_, :], None, bounds_check=TN - 1, oob_is_err=False, compute_op=ALU.add),
                       s_add, 32 * j + 16 * (a_ + 1), t, out_ok[-1], (s_add, 32 * j) if j else None)
            xg_free[j] = (t, (s_add, 32 * (j + 1)))

        for k in range(3):
            load_w(0, k)
        for k in range(NE):
            fill(k)
        load_xg(0)
        for k in range(3):
            load_w(1, k)
        load_xg(1)
        load_xg(2)
        split_w(0, 0)
        split_w(0, 1)
        turn_x(0)
        for j in range(NT):
            if j + 3 < NT:
                load_xg(j + 3)
            split_w(j + 1, 0)
            up_half(j, 0)
            if j + 1 < NT:
                turn_x(j + 1)
            split_w(j + 1, 1)
            split_h(j, 0)
            up_half(j, 1)
            split_w(j, 2)
            split_h(j, 1)
            if j:
                down(j - 1)
        down(NT - 1)
        SP.ops.append(("wait", s_add, 32 * NT))
        SP.ops.append(("wait", s_sc, sc_n[0]))
        SP.ops.append(("wait", s_out, 16 * NG))

        block = ctx.enter_context(nc.Block())

        @block.sync
        def _(eng):
            SP.play(eng)

        @block.tensor
        def _(eng):
            PE.play(eng)

        @block.vector
        def _(eng):
            DVE.play(eng)

        @block.scalar
        def _(eng):
            SC.play(eng)

        @block.gpsimd
        def _(eng):
            PL.play(eng)


def _lay(inputs):
    g = {k: np.asarray(v) for k, v in inputs.items()}
    wg = g["L0_ffn_w_gate"].transpose(0, 2, 1).reshape(NE, 2, 128, F).transpose(0, 2, 1, 3).reshape(NE, 128, 2 * F)
    wu = g["L0_ffn_w_up"].transpose(0, 2, 1).reshape(NE, 2, 128, F).transpose(0, 2, 1, 3).reshape(NE, 128, 2 * F)
    wn = g["L0_ffn_w_down"].transpose(0, 2, 1).reshape(NE, 4, 128, C).transpose(0, 2, 1, 3).reshape(NE, 128, 4 * C)
    a = {
        "x": g["x"], "ctxin": g["ctx_1024"],
        "lw": g["L0_attn_latent_w"].reshape(2, 128, L).transpose(1, 0, 2),
        "lb": g["L0_attn_latent_b"],
        "wd": g["L0_attn_Wd_w"].reshape(H, 2, 128, L).transpose(2, 1, 0, 3),
        "wdb": g["L0_attn_Wd_b"].T,
        "ow": g["L0_attn_out_w"].reshape(H, L, C).transpose(1, 0, 2),
        "ob": g["L0_attn_out_b"],
        "xw": g["L0_xattn_w"].reshape(2, 128).T,
        "xu": g["L0_xattn_u"].reshape(2, 128).T,
        "rw": g["L0_ffn_router_w"].T.reshape(2, 128, NE).transpose(1, 0, 2).reshape(128, 2 * NE),
        "wf": np.concatenate([wg, wu, wn], axis=2),
    }
    return {k: np.ascontiguousarray(v) for k, v in a.items()}


def kernel(**inputs):
    import concourse.bacc as bacc
    from concourse.bass_utils import run_bass_kernel_spmd as run

    nc = bacc.Bacc("TRN2", target_bir_lowering=False, num_devices=1)
    arrays = _lay(inputs)
    args = {n: nc.dram_tensor(n, a.shape, mybir.dt.from_np(a.dtype), kind="ExternalInput").ap() for n, a in arrays.items()}
    out = nc.dram_tensor("out", (B, T, C), mybir.dt.float32, kind="ExternalOutput").ap()
    xs = nc.dram_tensor("xs", (NE * CAP, RW), mybir.dt.float32, kind="Internal").ap()
    build(nc, **args, out=out, xs=xs)
    r = run(nc, [arrays], core_ids=[0])
    return r.results[0]["out"]
```

```python
import numpy as np
import concourse.bass as bass
from concourse import mybir
from contextlib import ExitStack

B, T, C = 16, 128, 256
H, L = 16, 72
NE, F = 8, 512
GB = 4
NG = B // GB
NU = NG * 16
EPS = 1e-5
TN = B * T
TW = 256
CAP = TN + TW
NT = (2 * TN + NE * (TW - 1)) // TW
PHASES = [-(-(2 * n - NE * (TW - 1)) // TW) for n in (TN * 3 // 4, TN * 7 // 8)] + [NT]
NX = 4
SHARE, SHARE_TILES = 0.9, 4.0
GAP, GAP_TILES = 5, 3
PACE, PACE_TILES = 1.0, 0.1
SCANS_FROM = 5


class Queue:

    def __init__(self, sem):
        self.sem, self.count, self.ops, self.met = sem, 0, [], {}

    def add(self, make, *waits, sig=True):
        need = {}
        for w in waits:
            if w is None:
                continue
            s, v = w
            need[id(s)] = (s, max(v, need.get(id(s), (s, 0))[1]))
        for s, v in need.values():
            if self.met.get(id(s), 0) < v:
                self.met[id(s)] = v
                self.ops.append(("wait", s, v))
        if sig:
            self.count += 1
        self.ops.append(("do", make, self.sem if sig else None))
        return (self.sem, self.count)

    def dma(self, make, sem, total, *waits):
        self.add(make, *waits, sig=False)
        self.ops[-1] = ("dma", make, sem)
        return (sem, total)

    def play(self, eng):
        for kind, a, b in self.ops:
            if kind == "wait":
                eng.wait_ge(a, b)
            elif kind == "dma":
                a(eng).then_inc(b, 16)
            else:
                i = a(eng)
                if b is not None:
                    i.then_inc(b, 1)


def build(nc, x, ctxin, lw, lb, wd, wdb, ow, ob, xw, xu, rw, wf, out, xs, xd):
    fp32 = mybir.dt.float32
    f32r = mybir.dt.float32r
    i32 = mybir.dt.int32
    ALU = mybir.AluOpType
    ACT = mybir.ActivationFunctionType
    AX = mybir.AxisListType

    ctx = ExitStack()
    with ctx:
        def sb(name, shape, dt=fp32, stack=ctx):
            return stack.enter_context(nc.sbuf_tensor(name, shape, dt))

        def sem(name):
            return ctx.enter_context(nc.semaphore(name))

        PE, DVE, SC, PL = (Queue(sem(n)) for n in ("s_pe", "s_dve", "s_act", "s_pool"))
        SP = Queue(sem("s_sp"))

        X = sb("X", [128, B, C])
        XN = sb("XN", [128, GB, C])
        EX = sb("EX", [128, GB, C])
        WK = [sb(f"WK{i}", [128, GB, C]) for i in range(2)]
        arena = sb("arena", [128, 3072])
        D0 = sb("D0", [128, 2, 517])
        ident = sb("ident", [128, 128])
        small = sb("small", [128, 1794])
        rwr = sb("rwr", [128, 2, 2, NE], f32r)
        xnTb = sb("xnTb", [128, 2, 2, 512], f32r)
        Utr = sb("Utr", [128, 128], f32r)
        onem = sb("onem", [128, 128], f32r)
        Mr = sb("Mr", [128, GB, NE], f32r)
        SL = sb("SL", [128, NG, 2, GB], i32)
        PI = sb("PI", [1, 2 * NT], i32)
        TKS = sb("TKS", [128, NG, 2, GB, 2])
        TK = sb("TK", [128, NT, 2, 2])
        with ExitStack() as s0:
            raw = sb("raw", [L, H * C], fp32, s0)
        cxa = sb("cxa", [128, 2048])
        CX = cxa[:, 0:1024].rearrange("p (b c) -> p b c", b=GB)
        XT3 = sb("XT3", [128, 2, 2, 512], f32r)
        s1 = ExitStack()
        xnTa = sb("xnTa", [128, 2, 2, 512], f32r, s1)
        Wd = sb("Wd", [128, 2, 2, H, L], f32r, s1)
        KT = [sb(f"KT{i}", [L, 2, 512], f32r, s1) for i in range(2)]
        V = [sb(f"V{i}", [128, 2, GB, L], f32r, s1) for i in range(2)]
        Vf = sb("Vf", [128, GB, L], fp32, s1)
        qT = [sb(f"qT{i}", [L, 2, 4, 512], f32r, s1) for i in range(2)]
        Ow = sb("Ow", [L, 2, H, C], f32r, s1)
        Lw = sb("Lw", [128, 2, 2, L], f32r, s1)
        obr = sb("obr", [1, 2, C], f32r, s1)
        onr = sb("onr", [1, 128], f32r, s1)
        EB = [sb(f"EB{i}", [128, 4, 128], fp32, s1) for i in range(2)]
        PT = sb("PT", [128, 2, 512], f32r, s1)
        ZT = sb("ZT", [L, 2, 512], f32r, s1)
        maskr = sb("maskr", [128, 4, 128], f32r, s1)
        identr = sb("identr", [128, 128], f32r, s1)
        s1.close()
        xnTs = [xnTa, xnTb]
        WF = [sb(f"WF{i}", [128, 2, 3072], f32r) for i in range(2)]
        WR = [arena, sb("WR1", [128, 3072])]
        XG = [cxa[:, 512 * i:512 * i + 512].rearrange("p (a c) -> p a c", a=2) for i in range(NX)]
        GT = [sb(f"GT{i}", [128, 2, 2, TW], f32r) for i in range(2)]
        SG = [sb(f"SG{i}", [128, 512]) for i in range(2)]
        HF = [sb(f"HF{i}", [128, 512]) for i in range(2)]
        HR = [sb(f"HR{i}", [128, 2, 4, TW], f32r) for i in range(2)]
        Y = [sb(f"Y{i}", [128, 2, C]) for i in range(2)]

        P = [ctx.enter_context(nc.psum_tensor(f"P{i}", [128, 512], fp32)) for i in range(6)]
        PO = ctx.enter_context(nc.psum_tensor("PO", [128, 2, 512], fp32))
        QB, SB, PTB, YB, TR = P[0], [P[1], P[2]], P[3], P[4], P[5]

        off = [0]

        def piece(n):
            off[0] += n
            return small[:, off[0] - n:off[0]]

        nm = piece(4)
        mv1 = piece(32).rearrange("p (b s) -> p b s", s=2)
        st = piece(24).rearrange("p (b s) -> p b s", s=6)
        rs1 = piece(16)
        ve = piece(16)
        tt = piece(16)
        mv2 = piece(8).rearrange("p (b s) -> p b s", s=2)
        rs2 = piece(4)
        nr = piece(4)
        mr = piece(4)
        NM = [piece(4) for _ in range(2)]
        SM = [piece(4) for _ in range(2)]
        lbc = piece(1)
        lbb = piece(L)
        wdb_s = piece(H)
        xws = piece(2)
        xus = piece(2)
        ew = piece(2)
        rwf = piece(16)
        rt = piece(14 * 32).rearrange("p (n b e) -> p n b e", n=14, e=NE)
        io = piece(32).rearrange("p (b e) -> p b e", e=NE)
        pos = piece(8)
        obf = piece(256)
        RUN = piece(NE)
        ecap = piece(NE)
        jio = piece(NT)
        big = piece(NT * NE).rearrange("p (j e) -> p j e", e=NE)
        big2 = piece(NT * NE).rearrange("p (j e) -> p j e", e=NE)
        pl = piece(16 * NE).rearrange("p (n e) -> p n e", e=NE)
        pj = piece(8 * NT).rearrange("p (n j) -> p n j", j=NT)
        assert off[0] <= 1794

        s_x = [sem(f"s_x{g}") for g in range(NG)]
        s_c = sem("s_c")
        s_w = [sem(f"s_w{i}") for i in range(6)]
        s_sc = [sem(f"s_sc{i}") for i in range(5)]
        s_fill = sem("s_fill")
        s_xd = [sem(f"s_xd{i}") for i in range(5)]
        s_tk = [sem(f"s_tk{i}") for i in range(4)]
        s_wf = [[sem(f"s_wf{i}_{k}") for k in range(3)] for i in range(2)]
        s_xg = [sem(f"s_xg{i}") for i in range(NX)]
        s_add = sem("s_add")
        s_out = [sem(f"s_out{i}") for i in range(5)]
        xv = x.rearrange("b t c -> t b c")
        cv = ctxin.rearrange("b t c -> t b c")
        x_in = []
        rWd = arena[:, 0:2304].rearrange("p (k h l) -> p k h l", k=2, h=H)
        rOw = raw[:, :].rearrange("p (h c) -> p h c", h=H)
        rLw = arena[:, 2304:2304 + 2 * L].rearrange("p (k l) -> p k l", k=2)

        def load_x(g):
            x_in.append(SP.dma(lambda e: e.dma_start(X[:, GB * g:GB * g + GB, :], xv[:, GB * g:GB * g + GB, :]), s_x[g], 16))

        load_x(0)
        n_small = 0
        for dst, src in ((lbc[0:L, :], lb.rearrange("(l a) -> l a", a=1)),
                         (lbb, lb.rearrange("(a l) -> a l", a=1).broadcast_to([128, L])),
                         (wdb_s[0:L, :], wdb), (xws, xw), (xus, xu), (rwf, rw),
                         (obf[0:1, :], ob.rearrange("(a c) -> a c", a=1)), (rLw, lw)):
            n_small += 16
            small_in = SP.dma(lambda e, d=dst, s=src: e.dma_start(d, s), s_w[0], n_small)
        small_in = (s_w[0], n_small)
        wd_in = SP.dma(lambda e: e.dma_start(rWd, wd), s_w[1], 16)
        ow_in = SP.dma(lambda e: e.dma_start(rOw, ow), s_w[2], 16)
        for g in range(1, NG):
            load_x(g)

        t = PL.add(lambda e: e.memset(ident[:, :], 0.0))
        ident_ok = PL.add(lambda e: e.affine_select(out=ident[:, :], in_=ident[:, :], compare_op=ALU.not_equal, fill=1.0,
                                                    base=0, pattern=[[-1, 128]], channel_multiplier=1), t)
        mf = EX[:, 0:2, :].rearrange("p a (b s) -> p (a b) s", s=128)
        t = PL.add(lambda e: e.memset(mf, 0.0))
        mask_f = PL.add(lambda e: e.affine_select(out=mf, in_=mf, compare_op=ALU.is_ge, fill=-float(2.0 ** 100),
                                                  base=0, pattern=[[0, 4], [-1, 128]], channel_multiplier=1), t)
        iota_ok = PL.add(lambda e: e.iota(io.bitcast(i32), pattern=[[0, GB], [1, NE]], base=0, channel_multiplier=0))
        ut_f = EX[:, 2, 0:128]
        t = PL.add(lambda e: e.memset(ut_f, 1.0))
        ut_ok = PL.add(lambda e: e.affine_select(out=ut_f, in_=ut_f, compare_op=ALU.is_gt, fill=0.0, base=0,
                                                 pattern=[[1, 128]], channel_multiplier=-1), t)
        on_f = PL.add(lambda e: e.memset(XN[:, 0, 0:128], 1.0))
        for g in range(NG):
            PL.add(lambda e, g=g: e.iota(TKS[:, g, :, :, 0].bitcast(i32), pattern=[[0, 2], [T, GB]], base=GB * T * g, channel_multiplier=1))
        PL.add(lambda e: e.iota(pl[:, 0, :].bitcast(i32), pattern=[[CAP, NE]], base=0, channel_multiplier=0))
        idx_ok = PL.add(lambda e: e.iota(pj[:, 0, :].bitcast(i32), pattern=[[1, NT]], base=0, channel_multiplier=0))

        pad = EX[:, 3, 0:144].rearrange("p (a c) -> p a c", c=2)
        t = PL.add(lambda e: e.memset(EX[:, 3, 0:144], 0.0))
        t = PL.add(lambda e: e.memset(pad[:, :, 0:1].bitcast(i32), TN), t)
        for k in range(2):
            SP.dma(lambda e, k=k: e.dma_start(xs.rearrange("(a p r) c -> a p (r c)", a=2, p=128)[k], EX[:, 3, 0:144]), s_fill, 16 * (k + 1), t)
        t = PL.add(lambda e: e.memset(WK[0][0:1, 0, :], 0.0))
        fill_ok = SP.dma(lambda e: e.dma_start(xd[TN:TN + 1, :], WK[0][0:1, 0, :]), s_fill, 48, t)

        def rest(n):
            if not state["rush"]:
                yield -max(1, round(n * state["pace"]))

        ev_ = {}

        def rsqrt(Q, v, y, n, *waits):
            t = Q.add(lambda e: e.tensor_scalar(y.bitcast(i32), v.bitcast(i32), -0.5, 1597463007.0, ALU.mult, ALU.add), *waits)
            h = Q.add(lambda e: e.tensor_scalar(v, v, -0.5, None, ALU.mult), t)
            for _ in range(3):
                t = Q.add(lambda e: e.tensor_tensor(tt[:, 0:n], y, y, ALU.mult), t)
                t = Q.add(lambda e: e.tensor_tensor(tt[:, 0:n], tt[:, 0:n], v, ALU.mult), t, h)
                t = Q.add(lambda e: e.tensor_scalar(tt[:, 0:n], tt[:, 0:n], 1.5, None, ALU.add), t)
                t = Q.add(lambda e: e.tensor_tensor(y, tt[:, 0:n], y, ALU.mult), t)
            return t

        def stats(b0, nb, mv, y, *waits, quick=False):
            for b in range(nb):
                ts = DVE.add(lambda e, b=b: e.bn_stats(st[:, b, :], X[:, b0 + b, :]), *waits)
                if b % 2:
                    yield 0.7
            for b in range(nb):
                t = DVE.add(lambda e, b=b: e.bn_aggr(mv[:, b, :], st[:, b, :]), ts)
            t = DVE.add(lambda e: e.tensor_scalar(ve[:, 0:nb], mv[:, 0:nb, 1], EPS, None, ALU.add), t, ev_.get("ve_free"))
            t = rsqrt(DVE if quick else PL, ve[:, 0:nb], y[:, 0:nb], nb, t)
            ev_["ve_free"] = t
            yield 0.5
            if not quick:
                yield from rest(5)
            return t

        def split(hi, lo, src, *waits):
            a = SC.add(lambda e: e.activation(hi, src, ACT.Copy), *waits)
            return a, DVE.add(lambda e: e.tensor_tensor(lo, src, hi.bitcast(fp32), ALU.subtract), a)

        def split_bias(hi, lo, src, bias, *waits):
            a = SC.add(lambda e: e.activation(hi, src, ACT.Identity, bias=bias), *waits)
            return a, DVE.add(lambda e: e.scalar_tensor_tensor(out=lo, in0=src, scalar=bias, in1=hi.bitcast(fp32),
                                                               op0=ALU.add, op1=ALU.subtract), a)

        def mm3(o, lt, rt_, start, stop, *waits, skip=False):
            for n, (a, b) in enumerate(((0, 0), (0, 1), (1, 0))):
                r = PE.add(lambda e, a=a, b=b, s=start and n == 0, z=stop and n == 2:
                           e.matmul(o, lt(a), rt_(b), start=s, stop=z, skip_group_check=skip),
                           *(waits if n == 0 else ()), sig=stop and n == 2)
            return r

        state = {"tr": [None, None], "xn": None}

        def tr_free():
            return state["tr"]

        now = [0]
        state.update(lock=False, rush=True, norm=False, route=False, tr_at=0, pace=PACE, share=SHARE, gap=GAP, quick=True, qb=())

        def tr_turn():
            while state["lock"] or (now[0] < state["tr_at"] and not state["rush"]):
                yield -1

        def own(it, *locks):
            while any(state[k] for k in locks):
                yield -1
            for k in locks:
                state[k] = True
            r = yield from it
            for k in locks:
                state[k] = False
            return r

        def tr_read(*readers):
            state["tr"] = list(readers)
            state["tr_at"] = now[0] + state["gap"]

        lw_ok = split(Lw[:, 0], Lw[:, 1], rLw, small_in)
        rw_ok = split(rwr[:, 0], rwr[:, 1], rwf.rearrange("p (k e) -> p k e", k=2), small_in)
        idr_ok = SC.add(lambda e: e.activation(identr[:, :], ident[:, :], ACT.Copy), ident_ok)
        mask_ok = SC.add(lambda e: e.activation(maskr[:, :, :], mf, ACT.Copy), mask_f)
        utr_ok = SC.add(lambda e: e.activation(Utr[:, :], ut_f, ACT.Copy), ut_ok)
        onem_ok = SC.add(lambda e: e.activation(onem[:, :], XN[:, 0, 0:128], ACT.Copy), on_f)
        on_ok = SC.add(lambda e: e.activation(onr[:, :], XN[0:1, 0, 0:128], ACT.Copy), on_f)
        ob_ok = split(obr[:, 0, :], obr[:, 1, :], obf[0:1, :], small_in)
        ew_ok = SC.add(lambda e: e.activation(ew, xws, ACT.Exp), small_in)
        eu_ok = SC.add(lambda e: e.activation(xus, xus, ACT.Exp), small_in)
        wdb_ok = DVE.add(lambda e: e.tensor_scalar(wdb_s[0:L, :], wdb_s[0:L, :], 0.25, None, ALU.mult), small_in)

        def d0_fill():
            d = []
            for k in range(2):
                d.append(PL.add(lambda e, k=k: e.tensor_scalar(D0[:, k, :], arena[:, 0:517], ew[:, k:k + 1], None, ALU.add), ew_ok, zero_ok))
            t = None
            for k in range(2):
                t = PL.add(lambda e, k=k: e.memset(D0[:, k, 0:517:129], 0.0), d[k])
            return t

        ln1 = {}
        last_q = {}
        kv = {}

        def ln1_stats(g):
            ln1[g] = yield from stats(GB * g, GB, mv1[:, GB * g:GB * g + GB, :], rs1[:, GB * g:GB * g + GB], x_in[g], quick=state["quick"])

        def transposed(dst, b0, nb, w_free, *more):
            done = []
            c = slice(128 * b0, 128 * (b0 + nb))
            for k in range(2):
                yield from tr_turn()
                for b in range(b0, b0 + nb):
                    p = PE.add(lambda e, b=b, k=k: e.transpose(TR[:, 128 * b:128 * b + 128], XN[:, b, 128 * k:128 * k + 128], ident[:, :]),
                               state["xn"], ident_ok, *tr_free(), sig=b == b0 + nb - 1)
                r = split(dst[:, 0, k, c], dst[:, 1, k, c], TR[:, c], p, w_free, *more)
                tr_read(*r)
                done += r
                yield 0.6 * nb / GB
            state["xn_free"] = [p]
            return done

        state["xn_free"] = [on_ok]

        def normalise(g, b0, nb, mv, y, *waits):
            t = DVE.add(lambda e: e.scalar_tensor_tensor(out=nm[:, 0:nb], in0=mv[:, 0:nb, 0], scalar=-1.0, in1=y[:, 0:nb], op0=ALU.mult, op1=ALU.mult),
                        *waits, state.get("nm_free"))
            for b in range(nb):
                t = SC.add(lambda e, b=b: e.activation(XN[:, b0 + b, :], X[:, GB * g + b0 + b, :], ACT.Identity, bias=nm[:, b:b + 1], scale=y[:, b:b + 1]),
                           *state["xn_free"], t)
                if b == 1:
                    yield from rest(2)
            state["xn"] = state["nm_free"] = ev_["xn_use"] = t

        def stage_a(g):
            xt = yield from own(a_norm(g), "norm")
            yield from a_kv(g, xt)

        def a_norm(g):
            if g not in ln1:
                yield from ln1_stats(g)
            yield from normalise(g, 0, GB, mv1[:, GB * g:GB * g + GB, :], rs1[:, GB * g:GB * g + GB], ln1[g])
            yield from rest(4)
            xnT = xnTs[g % 2]
            xt = yield from transposed(xnT, 0, GB, last_q.get(g - 2))
            yield from rest(2)
            xt_ok[g] = xt
            return xt

        def a_kv(g, xt):
            xnT = xnTs[g % 2]
            i = g % 2
            old = kv_free.get(g - 2, ())
            yield from rest(4)
            yield from tr_turn()
            for k in range(2):
                p = mm3(TR[0:L, :], lambda a, k=k: Lw[:, a, k, :], lambda a, k=k: xnT[:, a, k, :], k == 0, k == 1,
                        *xt, *lw_ok, *tr_free())
            kt = split_bias(KT[i][:, 0, :], KT[i][:, 1, :], TR[0:L, :], lbc[0:L, :], p, *old)
            tr_read(*kt)
            yield 0.7
            yield from tr_turn()
            state["lock"] = True
            for b in range(GB):
                if b == 2:
                    yield 0.1
                for k in range(2):
                    p = mm3(TR[:, L * b:L * b + L], lambda a, k=k, b=b: xnT[:, a, k, 128 * b:128 * b + 128],
                            lambda a, k=k: Lw[:, a, k, :], k == 0, k == 1, *tr_free())
            yield 0.1
            bb = lbb.unsqueeze(1).broadcast_to([128, GB, L])
            t = DVE.add(lambda e: e.tensor_tensor(Vf[:, :, :], TR[:, 0:GB * L].rearrange("p (b l) -> p b l", b=GB), bb, ALU.add),
                        p, small_in, state.get("vf_free"))
            tr_read(t)
            v = split(V[i][:, 0], V[i][:, 1], Vf[:, :, :], t, *old)
            state["vf_free"] = v[1]
            state["lock"] = False
            yield 0.8
            kv[g] = (kt, v)

        kv_free = {}
        xt_ok = {}

        q_ok = {}
        s_read = {}

        blocks = ([(g, hq, 0, GB) for g in range(3) for hq in range(4)]
                  + [(g, hq, b0, 2) for g in range(3, NG) for b0 in (0, 2) for hq in range(4)])
        units = [(k, g, hq, b0 + b) for k, (g, hq, b0, nb) in enumerate(blocks) for b in range(nb)]
        last_unit = {k: n for n, (k, *_) in enumerate(units)}
        assert len(units) == NU

        def q_head(k, j0, bank=None):
            g, hq, b0, nb = blocks[k]
            W, i = 128 * nb, k % 2
            xnT = xnTs[g % 2]
            Q, q_free = (QB, state["qb"]) if bank is None else (bank, state["q" + bank.name])
            c = slice(128 * b0, 128 * b0 + W)
            heads = range(j0, j0 + GB // nb)
            for m, j in enumerate(heads):
                for a_ in range(2):
                    p = mm3(Q[0:L, W * m:W * m + W], lambda a, k=a_, h=4 * hq + j: Wd[:, a, k, h, :], lambda a, k=a_: xnT[:, a, k, c], a_ == 0, a_ == 1,
                            *(wd_ok + xt_ok[g]), *q_free)
            last_q[g] = p
            hs = [(4 * hq + j, Q[0:L, W * m:W * m + W], qT[i][:, :, j, 0:W]) for m, j in enumerate(heads)]
            old = s_read.get(last_unit.get(k - 2))
            for h, src, dst in hs:
                r = SC.add(lambda e, h=h, src=src, dst=dst: e.activation(dst[:, 0, :], src, ACT.Identity, bias=wdb_s[0:L, h:h + 1]), p, wdb_ok, old)
            for h, src, dst in hs:
                v = DVE.add(lambda e, h=h, src=src, dst=dst: e.scalar_tensor_tensor(out=dst[:, 1, :], in0=src, scalar=wdb_s[0:L, h:h + 1],
                                                                                    in1=dst[:, 0, :].bitcast(fp32), op0=ALU.add, op1=ALU.subtract), r)
            r = (r, v)
            q_ok.setdefault(k, []).extend(r)
            state["qb" if bank is None else "q" + bank.name] = r

        q_steps = {}
        for k in range(1, len(blocks)):
            a, b = max(0, last_unit.get(k - 2, 0)), last_unit[k - 1] - 1
            w = GB // blocks[k][3]
            jobs = list(range(0, 4, w))
            for m, j in enumerate(jobs):
                q_steps.setdefault(min(b, a + m), []).append((k, j))

        ep, ev, FA, FB, FC = (arena[:, 518 * i:518 * i + 517] for i in range(5))
        cu, cw = cxa[:, 1024:1536], cxa[:, 1536:2048]
        epv = ep[:, 0:516].rearrange("p (b j) -> p b j", j=129)[:, :, 1:129]
        evv = ev[:, 0:516].rearrange("p (b j) -> p b j", j=129)[:, :, 1:129]
        cuv, cwv = (a[:, 0:512].rearrange("p (b j) -> p b j", j=128) for a in (cu, cw))
        wk_free = {}
        wk_ok = {}
        e_done, w_done = set(), set()
        ar = {"f": (), "s": None}

        def fwd(a):
            return a[:, 0:516].rearrange("p (b j) -> p b j", j=129)[:, :, 0:128]

        def bwd(a):
            return a[:, 1:517].rearrange("p (b j) -> p b j", j=129)[:, :, 1:129]

        def stage_w(g, k):
            while len(ctx_in) <= g:
                yield -1
            yield from tr_turn()
            cin = ctx_in[g]
            tv = TR[:, :].rearrange("p (b j) -> p b j", j=128)
            for b in range(GB):
                p = PE.add(lambda e, b=b: e.transpose(TR[:, 128 * b:128 * b + 128], CX[:, b, 128 * k:128 * k + 128], ident[:, :]),
                           cin, ident_ok, *tr_free(), sig=b == GB - 1)
            if k == 1 and g + 1 < NG:
                ctx_in.append(SP.dma(lambda e: e.dma_start(CX, cv[:, GB * (g + 1):GB * (g + 2), :]), s_c, 16 * (g + 2), p))
            a1 = SC.add(lambda e: e.activation(epv, tv, ACT.Exp), p, d0_ok, *ar["f"])
            d1 = DVE.add(lambda e: e.tensor_tensor(evv, tv, epv, ALU.mult), a1)
            tr_read(d1)
            yield 0.6
            yield from rest(2)
            a2 = SC.add(lambda e: e.activation(cuv, epv, ACT.Copy, scale=xus[:, k:k + 1]), a1, eu_ok)
            f1 = DVE.add(lambda e: e.tensor_tensor_scan(FA, D0[:, k, :], ep, 0.0, ALU.mult, ALU.add), d0_ok, a1, *ar["f"])
            yield 0.6
            f2 = DVE.add(lambda e: e.tensor_tensor_scan(FB[:, ::-1], D0[:, k, ::-1], ep[:, ::-1], 0.0, ALU.mult, ALU.add))
            yield 0.6
            p1 = PL.add(lambda e: e.tensor_tensor(cuv, cuv, fwd(FA), ALU.add), f1, a2)
            d2 = SC.add(lambda e: e.activation(cwv, evv, ACT.Copy, scale=xus[:, k:k + 1]), d1)
            g1 = DVE.add(lambda e: e.tensor_tensor_scan(FC, D0[:, k, :], ev, 0.0, ALU.mult, ALU.add), d1)
            yield 0.6
            yield from rest(2)
            p2 = PL.add(lambda e: e.tensor_tensor(cuv, cuv, bwd(FB), ALU.add), f2, p1)
            g2 = DVE.add(lambda e: e.tensor_tensor_scan(FA[:, ::-1], D0[:, k, ::-1], ev[:, ::-1], 0.0, ALU.mult, ALU.add), p1)
            yield 0.6
            yield from rest(3)
            p3 = PL.add(lambda e: e.tensor_tensor(cwv, cwv, fwd(FC), ALU.add), g1, d2)
            for b in range(2):
                r = DVE.add(lambda e, b=b: e.reciprocal(cuv[:, b, :], cuv[:, b, :]), p2)
                yield 0.85
            p4 = PL.add(lambda e: e.tensor_tensor(cwv, cwv, bwd(FA), ALU.add), g2, p3)
            for b in range(2, 4):
                r = DVE.add(lambda e, b=b: e.reciprocal(cuv[:, b, :], cuv[:, b, :]), p2)
                yield 0.85
            yield from rest(2)
            p5 = PL.add(lambda e: e.tensor_tensor(cwv, cwv, cuv, ALU.mult), r, p4)
            yield from rest(7)
            while g >= 2 and g - 2 not in e_done:
                yield -1
            yield from tr_turn()
            for b in range(GB):
                p = PE.add(lambda e, b=b: e.transpose(TR[:, 128 * b:128 * b + 128], cwv[:, b, :], ident[:, :]),
                           p5, *tr_free(), sig=b == GB - 1)
            a = SC.add(lambda e: e.activation(WK[g % 2][:, :, 128 * k:128 * k + 128], tv, ACT.Copy, scale=0.5), p, wk_free.get(g % 2), fill_ok)
            tr_read(a)
            wk_ok[g] = a
            yield 0.1
            ar["f"] = (p, g2, p5)

        exp_ok, p_ok, pt_ok, y_done, z_ok, o_done, t_done = {}, {}, {}, {}, {}, {}, {}

        def stage_s(n):
            kb, g, hq, b = units[n]
            i, S = kb % 2, SB[n % 2]
            c = 128 * (b - blocks[kb][2])
            k = KT[g % 2]
            p = PE.add(lambda e: e.matmul(S[:, :], identr[:, :], maskr[:, :, :].rearrange("p a b -> p (a b)"), start=True, stop=False,
                                          skip_group_check=True), idr_ok, mask_ok, exp_ok.get(n - 2), sig=False)
            for j in range(4):
                p = mm3(S[:, 128 * j:128 * j + 128], lambda a, j=j: qT[i][:, a, j, c:c + 128],
                        lambda a: k[:, a, 128 * b:128 * b + 128], False, True, *(q_ok[kb] + list(kv[g][0]) if j == 0 else ()), skip=True)
            s_read[n] = p
            Sv = S[:, :].rearrange("p (h s) -> p h s", h=4)
            d = DVE.add(lambda e: e.tensor_reduce(NM[n % 2], Sv, AX.X, ALU.max, negate=True), p, exp_ok.get(n - 2))
            for j in range(4):
                a = SC.add(lambda e, j=j: e.activation(EB[n % 2][:, j, :], S[:, 128 * j:128 * j + 128], ACT.Exp, bias=NM[n % 2][:, j:j + 1],
                                                       accum_out=SM[n % 2][:, j:j + 1]), d, t_done.get(n - 2), p_ok.get(n - 2))
            exp_ok[n] = a

        def stage_n(n):
            d = DVE.add(lambda e: e.reciprocal(SM[n % 2], SM[n % 2]), exp_ok[n])
            p_ok[n] = PL.add(lambda e: e.tensor_tensor(EB[n % 2][:, :, :], EB[n % 2][:, :, :],
                                                       SM[n % 2].unsqueeze(2).broadcast_to([128, 4, 128]), ALU.mult), d)

        def stage_t(n):
            for j in range(4):
                p = PE.add(lambda e, j=j: e.transpose(PTB[:, 128 * j:128 * j + 128], EB[n % 2][:, j, :], ident[:, :]),
                           p_ok[n], ident_ok, *pt_ok.get(n - 1, ()), sig=j == 3)
            t_done[n] = p
            pt_ok[n] = split(PT[:, 0, :], PT[:, 1, :], PTB[:, :], p, y_done.get(n - 1))

        def stage_y(n):
            _, g, hq, b = units[n]
            v = V[g % 2]
            y_done[n] = mm3(YB[0:L, :], lambda a: v[:, a, b, :], lambda a: PT[:, a, :], True, True,
                            *pt_ok[n], *kv[g][1], *z_ok.get(n - 1, z_first))
            kv_free[g] = (s_read[n], y_done[n])
            z_ok[n] = split(ZT[:, 0, :], ZT[:, 1, :], YB[0:L, :], y_done[n], o_done.get(n - 1))

        def stage_o(n):
            _, g, hq, b = units[n]
            o = PO[:, b // 2, 256 * (b % 2):256 * (b % 2) + 256]
            if hq == 0:
                for a in range(2):
                    PE.add(lambda e, a=a: e.matmul(o, onr[:, :], obr[:, a, :], start=a == 0 and b % 2 == 0, stop=False, skip_group_check=True),
                           on_ok, *ob_ok, state.get("o_free"), sig=False)
            for j in range(4):
                h = 4 * hq + j
                p = mm3(o, lambda a, j=j: ZT[:, a, 128 * j:128 * j + 128], lambda a, h=h: Ow[:, a, h, :], False, j == 3,
                        *z_ok[n], *ow_ok[hq], skip=True)
            o_done[n] = p

        def e_add(g, b0, nb):
            v = X[:, GB * g + b0:GB * g + b0 + nb, :].rearrange("p (a b) c -> p a (b c)", b=2)
            t = DVE.add(lambda e: e.tensor_tensor(v, PO[:, b0 // 2:(b0 + nb) // 2, :], v, ALU.add), ev_["o"])
            state["o_free"] = t
            ev_["x1", g, b0] = t

        def e_ln2(g, b0, nb):
            t = yield from stats(GB * g + b0, nb, mv2, rs2, ev_["x1", g, b0], ev_.get("nr_free"), ev_.get("xn_use"), quick=state["quick"])
            DVE.add(lambda e: e.tensor_scalar(nr, rs2, 0.5, None, ALU.mult), t)
            ev_["nr"] = DVE.add(lambda e: e.scalar_tensor_tensor(out=mr[:, 0:nb], in0=mv2[:, 0:nb, 0], scalar=-0.5, in1=rs2[:, 0:nb],
                                                                 op0=ALU.mult, op1=ALU.mult), t)

        def e_sig(g, b0, nb):
            while g not in w_done:
                yield -1
            for b in range(b0, b0 + nb, 2):
                for b_ in (b, b + 1):
                    a = SC.add(lambda e, b=b_: e.activation(EX[:, b, :], X[:, GB * g + b, :], ACT.Tanh, bias=mr[:, b - b0:b - b0 + 1], scale=nr[:, b - b0:b - b0 + 1]),
                               ev_["nr"], mask_ok, utr_ok, fill_ok, ev_.get(("x2", b)))
                yield -2
                d = DVE.add(lambda e, b=b: e.scalar_tensor_tensor(out=EX[:, b:b + 2, :], in0=EX[:, b:b + 2, :], scalar=1.0,
                                                                  in1=WK[g % 2][:, b:b + 2, :], op0=ALU.add, op1=ALU.mult), a, wk_ok[g])
                q = DVE if state["quick"] else PL
                ev_["x2", b] = ev_["x2"] = q.add(lambda e, b=b: e.tensor_tensor(X[:, GB * g + b:GB * g + b + 2, :], X[:, GB * g + b:GB * g + b + 2, :],
                                                                                EX[:, b:b + 2, :], ALU.add), d)
                yield 0.6 if nb == GB else 1.2
            ev_["nr_free"] = a
            wk_free[g % 2] = d
            if b0 + nb == GB:
                e_done.add(g)

        def e_ln3(g, b0, nb):
            t = yield from stats(GB * g + b0, nb, mv2, rs2, ev_["x2"], ev_["nr_free"], ev_.get("xn_use"), quick=state["quick"])
            yield from normalise(g, b0, nb, mv2, rs2, t)
            r0 = T * (GB * g + b0)
            xd_ok[g + b0 // 2] = SP.dma(lambda e: e.dma_start(xd[r0:r0 + T * nb, :].rearrange("(b t) c -> t b c", t=T), XN[:, b0:b0 + nb, :]),
                                        s_xd[g + b0 // 2], 16, state["xn"])
            yield from rest(4)
            xt3 = yield from transposed(XT3, b0, nb, ev_.get("xt3_free"), *ow_ok[3])
            state["xn_free"].append(xd_ok[g + b0 // 2])
            return xt3

        xd_ok, sc_ok, out_ok = {}, {}, {}

        def e_xt(g, b0, nb, xt3):
            yield from rest(4)
            yield from tr_turn()
            state["lock"] = True
            for b in range(b0, b0 + nb):
                for k in range(2):
                    p = mm3(TR[:, NE * b:NE * b + NE], lambda a, k=k, b=b: XT3[:, a, k, 128 * b:128 * b + 128],
                            lambda a, k=k: rwr[:, a, k, :], k == 0, k == 1, *xt3, *rw_ok, *tr_free())
                if b % 2:
                    yield 0.1
            ev_["xt3_free"] = p
            t = DVE.add(lambda e: e.tensor_copy(rt[:, 6, 0:nb, :], TR[:, NE * b0:NE * (b0 + nb)].rearrange("p (b e) -> p b e", e=NE)), p)
            tr_read(t)
            ev_["lg"] = t
            state["lock"] = False

        def router(g, b0, nb):
            OH, S2, E2, FD, KE, PR = (rt[:, 2 * i:2 * i + 2, 0:nb, :] for i in (2, 3, 4, 5, 0, 1))
            s, s2, oh1, oh2 = S2[:, 0], S2[:, 1], OH[:, 0], OH[:, 1]
            a1, key, ab = PR[:, 0], PR[:, 1], rt[:, 12, 0:nb, :]
            rd = rt[:, 13].rearrange("p b e -> p (b e)").rearrange("p (n c b) -> p n c b", n=4, c=2)
            M, I, Z, SF = (rd[:, i, :, 0:nb] for i in range(4))
            add = DVE.add

            def bc(a):
                return a.unsqueeze(2).broadcast_to([128, nb, NE])

            def bc2(a):
                return a.unsqueeze(3).broadcast_to([128, 2, nb, NE])

            def twice(a):
                return a.unsqueeze(1).broadcast_to([128, 2, nb, NE])

            def tt_(o, p, q, op, *w):
                return add(lambda e: e.tensor_tensor(o, p, q, op), *w)

            def stt(o, p, sc, q, op0, op1, *w):
                return add(lambda e: e.scalar_tensor_tensor(out=o, in0=p, scalar=sc, in1=q, op0=op0, op1=op1), *w)

            io_ = ios[:, 0:nb, :]

            def first_max(sc, m, i, oh, *w):
                t = add(lambda e: e.tensor_reduce(m, sc, AX.X, ALU.max), *w)
                t = tt_(a1, sc, bc(m), ALU.is_lt, t)
                t = stt(key, a1, float(NE), io_, ALU.mult, ALU.add, t)
                t = add(lambda e: e.tensor_reduce(i, key, AX.X, ALU.min), t)
                return tt_(oh, io_, bc(i), ALU.is_equal, t)

            n_abs = add(lambda e: e.tensor_scalar(ab, s, -1.0, None, ALU.mult), ev_["lg"])
            o1 = first_max(s, M[:, 0], I[:, 0], oh1, ev_["lg"], ios_ok)
            n_abs = tt_(ab, ab, s, ALU.max, n_abs)
            yield 1.2
            t = stt(s2, oh1, -3.0e38, s, ALU.mult, ALU.add, o1)
            o2 = first_max(s2, M[:, 1], I[:, 1], oh2, t)
            m = tt_(Mr[:, 0:nb, :], oh1, oh2, ALU.add, o2, ev_.get("m_free"))
            m8 = tt_(E2, S2, bc2(M), ALU.subtract, o2)
            x_ = SC.add(lambda e: e.activation(E2, E2, ACT.Exp), m8)
            yield 1.5
            yield from rest(3)
            yield from tr_turn()
            PE.add(lambda e: e.matmul(TR[:, 0:NE * nb], Utr[:, :], Mr[:, 0:nb, :].rearrange("p b e -> p (b e)"), start=True, stop=False, skip_group_check=True),
                   m, utr_ok, *tr_free(), sig=False)
            for b in range(1, nb + 1):
                for b_ in range(b):
                    z = b == nb and b_ == b - 1
                    p = PE.add(lambda e, b=b, b_=b_, z=z: e.matmul(TR[:, NE * b:NE * b + NE], onem[:, :], Mr[:, b_, :], start=False, stop=z,
                                                                   skip_group_check=True), onem_ok, sig=z)
            ev_["m_free"] = p
            f = tt_(FD, twice(ab), bc2(M), ALU.max, n_abs, o2)
            d = tt_(KE, bc2(M), twice(s), ALU.subtract, o2)
            f = stt(KE, FD, 0.02, KE, ALU.mult, ALU.is_ge, f, d)
            run = RUN.unsqueeze(1).broadcast_to([128, nb, NE])
            t = tt_(key, TR[:, 0:NE * nb].rearrange("p (b e) -> p b e", e=NE), run, ALU.add, p, ev_["run"])
            ev_["run"] = tt_(RUN, RUN, TR[:, NE * nb:NE * nb + NE], ALU.add, t)
            tr_read(ev_["run"])
            t = tt_(FD, OH, twice(key), ALU.mult, t, f)
            t = add(lambda e: e.tensor_reduce(SF, FD, AX.X, ALU.add), t)
            sl = add(lambda e: e.tensor_copy(SL[:, g, :, b0:b0 + nb], SF), t)
            f = tt_(E2, E2, KE, ALU.mult, x_, f)
            f = add(lambda e: e.tensor_reduce(Z, E2, AX.X, ALU.add), f)
            w = add(lambda e: e.reciprocal(TKS[:, g, :, b0:b0 + nb, 1], Z), f)
            yield 1.9
            i = g + b0 // 2
            for c in range(2):
                for b in range(b0, b0 + nb):
                    sc_ok[i] = PL.dma(lambda e, b=b, c=c: e.indirect_dma_start(xs, bass.IndirectOffsetOnAxis(ap=SL[:, g, c, b:b + 1], axis=0),
                                                                               TKS[:, g, c, b, :], None),
                                      s_sc[i], 16 * (nb * c + b - b0 + 1), sl, w, idx_ok, fill_ok)
                    if b % 2:
                        yield from rest(2)

        plan_ok = {}

        def phase(j):
            return sum(j >= z for z in PHASES)

        def plan(i):
            add = DVE.add
            second = i == 2
            j0 = PHASES[i - 1] if i else 0
            n = PHASES[i] - j0
            nf, tl, te, one, first, m, v = (pl[0:1, i, :] for i in range(1, 8))
            eid, rs, un, tmp = (pj[0:1, i, 0:n] for i in range(1, 5))
            cmp, sel = big[0:1, 0:n, :], big2[0:1, 0:n, :]
            jb = jio[0:1, 0:n]
            o1 = add(lambda e: e.memset(one, 1.0), ev_["run"])
            t = add(lambda e: e.scalar_tensor_tensor(out=nf, in0=RUN[0:1, :], scalar=float(TW - 1) if second else 0.0, in1=ecap[0:1, :],
                                                     op0=ALU.add, op1=ALU.subtract), ev_["run"])
            t = add(lambda e: e.tensor_copy(tl.bitcast(i32), nf), t)
            t = add(lambda e: e.tensor_scalar(tl.bitcast(i32), tl.bitcast(i32), 8, None, ALU.logical_shift_right), t)
            t = add(lambda e: e.tensor_copy(nf, tl.bitcast(i32)), t)
            if i:
                t = add(lambda e: e.tensor_tensor(nf, nf, first, ALU.subtract), t, plan_ok["first"])
            te_ok = add(lambda e: e.tensor_tensor_scan(te, one, nf, 0.0, ALU.mult, ALU.add), t, o1)
            yield 2.0
            t = add(lambda e: e.tensor_tensor(v, nf, te, ALU.subtract), te_ok)
            if i:
                t = add(lambda e: e.tensor_tensor(v, v, first, ALU.add), t)
            if not second:
                t_ = add(lambda e: e.tensor_scalar(m, te, float(n), None, ALU.min), t)
                if i:
                    t_ = add(lambda e: e.tensor_tensor(first, first, m, ALU.add), t_)
                else:
                    t_ = add(lambda e: e.tensor_copy(first, m), t_)
                plan_ok["first"] = add(lambda e: e.tensor_tensor(first[:, 1:NE], first[:, 1:NE], m[:, 0:NE - 1], ALU.subtract), t_)
            v_ok = add(lambda e: e.scalar_tensor_tensor(out=v, in0=v, scalar=float(TW), in1=ecap[0:1, :], op0=ALU.mult, op1=ALU.add), t)
            t = add(lambda e: e.tensor_tensor(cmp, te.unsqueeze(1).broadcast_to([1, n, NE]), jb.unsqueeze(2).broadcast_to([1, n, NE]), ALU.is_le), te_ok)
            t1 = add(lambda e: e.tensor_reduce(eid, cmp, AX.X, ALU.add), t)
            t4 = add(lambda e: e.tensor_scalar(un, eid, float(NE), None, ALU.is_ge), t1)
            t5 = add(lambda e: e.tensor_scalar(eid, eid, float(NE - 1), None, ALU.min), t4)
            ie = add(lambda e: e.tensor_copy(PI[0:1, j0:j0 + n], eid), t5)
            t = add(lambda e: e.tensor_tensor(cmp, ios[0:1, 0, :].unsqueeze(1).broadcast_to([1, n, NE]), eid.unsqueeze(2).broadcast_to([1, n, NE]),
                                              ALU.is_equal), t5)
            t = add(lambda e: e.tensor_tensor(sel, cmp, v.unsqueeze(1).broadcast_to([1, n, NE]), ALU.mult), t, v_ok)
            t = add(lambda e: e.tensor_reduce(rs, sel, AX.X, ALU.add), t)
            t = add(lambda e: e.scalar_tensor_tensor(out=rs, in0=jb, scalar=float(TW), in1=rs, op0=ALU.mult, op1=ALU.add), t)
            t = add(lambda e: e.tensor_scalar(tmp, rs, -1.0, RUN[0:1, NE - 1:NE], ALU.mult, ALU.add), t)
            t = add(lambda e: e.tensor_tensor(tmp, tmp, un, ALU.mult), t)
            t = add(lambda e: e.tensor_tensor(rs, rs, tmp, ALU.add), t)
            plan_ok[i] = (ie, add(lambda e: e.tensor_copy(PI[0:1, NT + j0:NT + j0 + n], rs), t))
            yield 2.0

        ios = piece(32).rearrange("p (b e) -> p b e", e=NE)
        ios_ok = DVE.add(lambda e: e.tensor_copy(ios, io.bitcast(i32)), iota_ok)
        DVE.add(lambda e: e.tensor_copy(ecap, pl[:, 0, :].bitcast(i32)), idx_ok)
        DVE.add(lambda e: e.tensor_copy(jio, pj[:, 0, :].bitcast(i32)), idx_ok)
        ev_["run"] = DVE.add(lambda e: e.tensor_copy(RUN, pl[:, 0, :].bitcast(i32)), idx_ok)

        ctx_in = []
        def run_all(it):
            for _ in it:
                pass

        wd_ok = [SC.add(lambda e: e.activation(Wd[:, 0], rWd, ACT.Copy, scale=0.25), wd_in)]
        wd_ok.append(DVE.add(lambda e: e.scalar_tensor_tensor(out=Wd[:, 1].rearrange("p k h l -> p (k h l)"),
                                                              in0=rWd.rearrange("p k h l -> p (k h l)"), scalar=0.25,
                                                              in1=Wd[:, 0].bitcast(fp32).rearrange("p k h l -> p (k h l)"),
                                                              op0=ALU.mult, op1=ALU.subtract), wd_ok[0]))
        run_all(stage_a(0))
        zero_ok = PL.add(lambda e: e.memset(arena[:, :], 0.0), *wd_ok, *lw_ok)
        d0_ok = d0_fill()
        for j in range(4):
            state["q" + YB.name] = state.get("q" + YB.name, ())
            q_head(0, j, YB if j % 2 else None)
        ow_ok, z_first = [], state["q" + YB.name]

        def split_ow():
            for h in range(0, H, 4):
                ow_ok.append(split(Ow[:, 0, h:h + 4, :], Ow[:, 1, h:h + 4, :], rOw[:, h:h + 4, :], ow_in))
                yield

        def first():
            yield from split_ow()
            ctx_in.append(SP.dma(lambda e: e.dma_start(CX, cv[:, 0:GB, :]), s_c, 16, *[t for pair in ow_ok for t in pair]))

        def both_w(g):
            yield from stage_w(g, 0)
            yield from stage_w(g, 1)
            w_done.add(g)

        ov = out.rearrange("b t c -> t b c")

        def e_route(g, b0, nb, xt3):
            yield from e_xt(g, b0, nb, xt3)
            yield
            yield from router(g, b0, nb)
            if g == NG - 1:
                yield from plan(1 + b0 // 2)

        def stage_e(g, b0, nb):
            while g + b0 // 2 > 0 and g + b0 // 2 - 1 not in xd_ok:
                yield -1
            yield from own(e_ln2(g, b0, nb), "norm")
            yield
            yield from e_sig(g, b0, nb)
            yield from rest(5)
            lo, hi = GB * g + b0, GB * g + b0 + nb
            i = g + b0 // 2
            out_ok[i] = SP.dma(lambda e: e.dma_start(ov[:, lo:hi, :], X[:, lo:hi, :]), s_out[i], 16, ev_["x2"])
            xt3 = yield from own(e_ln3(g, b0, nb), "norm")
            yield from own(e_route(g, b0, nb, xt3), "route")

        GP, UP, TG = [P[0], P[1]], [P[2], P[3]], P[4]
        outr = out.rearrange("b t c -> (b t) c")
        parts = ((0, 1024), (1024, 2048), (2048, 3072))
        w_in, w_ok, w_free, raw_free = {}, {}, {}, {}
        xg_in, gt_ok, gt_free, xg_free = {}, {}, {}, {}
        g_read, h_ok, h_free, o_read, y_ok, up_done = {}, {}, {}, {}, {}, {}

        waiting = []
        att_done = ()

        def scans_done():
            assert NG - 1 in w_done
            return ar["f"]

        def ready(j):
            return phase(j) in plan_ok

        def load_w(j, k):
            i, (a, b) = j % 2, parts[k]
            if j >= NT:
                return
            if not ready(j):
                waiting.append((j, k))
                return

            def make(e):
                v = e.value_load(PI[0:1, j:j + 1], min_val=0, max_val=NE - 1)
                return e.dma_start(WR[i][:, a:b], wf[bass.ds(v, 1), :, a:b].rearrange("a p n -> (a p) n"))

            w_in[j, k] = SP.dma(make, s_wf[i][k], 16 * (j // 2 + 1), plan_ok[phase(j)][0], *(att_done if i else scans_done()), *raw_free.get((j - 2, k), ()))

        tk_in = {}

        def load_tk(j):
            def make(e):
                v = e.value_load(PI[0:1, NT + j:NT + j + 1], min_val=0, max_val=NE * CAP - TW)
                return e.dma_start(TK[:, j, :, :], xs[bass.ds(v, TW), :].rearrange("(p a) c -> p a c", a=2))

            tk_in[j] = SP.dma(make, s_tk[j % 4], 16 * (j // 4 + 1), plan_ok[phase(j)][1], *list(sc_ok.values())[:3 + phase(j)], fill_ok, tk_in.get(j - 4))

        def load_xg(j):
            i = j % NX
            for a_ in range(2):
                xg_in[j] = PL.dma(lambda e, a_=a_: e.indirect_dma_start(XG[i][:, a_, :], None, xd[0:(TN * 3 // 4, TN * 7 // 8, TN + 1)[phase(j)], :], bass.IndirectOffsetOnAxis(ap=TK[:, j, a_, 0:1].bitcast(i32), axis=0)),
                                  s_xg[i], 32 * (j // NX) + 16 * (a_ + 1), tk_in[j], *list(xd_ok.values())[:3 + phase(j)], fill_ok, *scans_done(), xg_free.get(j - NX))

        beside = [[(0, first()), (0, stage_a(1)), (0, own(ln1_stats(2), "norm")), (0, own(ln1_stats(3), "norm")), (19, stage_a(2)), (35, stage_a(3))],
                  [(19, stage_e(0, 0, GB)), (35, stage_e(1, 0, GB)),
                   (51, stage_e(2, 0, GB)), (51, plan(0)), (59, stage_e(3, 0, 2))],
                  [(NU + 3, stage_e(3, 2, 2))],
                  [(SCANS_FROM, both_w(0)), (SCANS_FROM, both_w(1)), (1, both_w(2)), (1, both_w(3))]]
        credit, wake = [0.0], [0, 0, 0, 0]
        state.update(rush=False, quick=False)

        def turn(n, k=1):
            for _ in range(k):
                now[0] += 1
                credit[0] = min(credit[0] + state["share"], state["share"] + 0.1)
                for i, parts_ in enumerate(beside):
                    while credit[0] > 0 and parts_ and parts_[0][0] <= n and wake[i] <= now[0]:
                        c = next(parts_[0][1], "end")
                        if c == "end":
                            parts_.pop(0)
                        elif c is not None and c < 0:
                            wake[i] = now[0] - c
                        else:
                            credit[0] -= c or 0.6

        def finish(n, until):
            state["rush"] = True
            while not until():
                assert any(p and p[0][0] <= n for p in beside)
                for i, parts_ in enumerate(beside):
                    if parts_ and parts_[0][0] <= n and next(parts_[0][1], "end") == "end":
                        parts_.pop(0)
            state["rush"] = False

        for n in range(NU + 3):
            if 2 <= n < NU + 2:
                stage_t(n - 2)
            if n < NU:
                stage_s(n)
            turn(n)
            for job in q_steps.get(n, ())[:1]:
                q_head(*job)
            turn(n)
            if n >= 3:
                stage_o(n - 3)
                k, g, hq, b = units[n - 3]
                if hq == 3 and n - 3 == last_unit[k]:
                    ev_["o"] = o_done[n - 3]
                    e_add(g, blocks[k][2], blocks[k][3])
            for job in q_steps.get(n, ())[1:]:
                q_head(*job)
            turn(n)
            if n < NU:
                stage_n(n)
            if 2 <= n < NU + 2:
                stage_y(n - 2)
            turn(n, 2)
            if n == NU:
                for j in range(3):
                    load_xg(j)
            if n == NU - 1 or (n > 58 and 0 in plan_ok and not w_in):
                finish(n, lambda: 0 in plan_ok and NG - 1 in w_done)
                if not w_in:
                    for j in range(3):
                        load_tk(j)
                    for k in range(3):
                        load_w(0, k)

        att_done = (o_done[NU - 1], (SC.sem, SC.count), (DVE.sem, DVE.count), (PL.sem, PL.count))

        state.update(quick=True, pace=PACE_TILES, share=SHARE_TILES, gap=GAP_TILES)

        def split_w(j, k):
            i, (a, b) = j % 2, parts[k]
            if j >= NT:
                return
            h = SC.add(lambda e: e.activation(WF[i][:, 0, a:b], WR[i][:, a:b], ACT.Copy), w_in[j, k],
                       (w_free if k == 2 else up_done).get(j - 2))
            t = DVE.add(lambda e: e.tensor_tensor(WF[i][:, 1, a:b], WR[i][:, a:b], WF[i][:, 0, a:b].bitcast(fp32), ALU.subtract), h)
            w_ok[j, k] = raw_free[j, k] = (h, t)
            load_w(j + 2, k)

        def turn_x(j):
            for k in range(2):
                for a in range(2):
                    p = PE.add(lambda e, k=k, a=a: e.transpose(TG[:, 256 * k + 128 * a:256 * k + 128 * a + 128],
                                                               XG[j % NX][:, a, 128 * k:128 * k + 128], ident[:, :]),
                               xg_in[j], *gt_ok.get(j - 1, ()), sig=k + a == 2)
            xg_free[j] = p
            o = GT[j % 2]
            gt_ok[j] = split(o[:, 0, :, :], o[:, 1, :, :], TG[:, :].rearrange("p (k t) -> p k t", k=2), p, up_done.get(j - 2))

        def up_half(j, n):
            w, x_ = WF[j % 2], GT[j % 2]
            gate = w[:, :, 0:1024].rearrange("p a (k f) -> p a k f", k=2)
            up = w[:, :, 1024:2048].rearrange("p a (k f) -> p a k f", k=2)
            u = 2 * j + n
            res = []
            for bank, m, k0 in ((GP[n], gate, 0), (UP[n], up, 1)):
                for q in range(2):
                    fc = 2 * n + q
                    for k in range(2):
                        p = mm3(bank[:, TW * q:TW * q + TW], lambda a, k=k, fc=fc, m=m: m[:, a, k, 128 * fc:128 * fc + 128],
                                lambda a, k=k: x_[:, a, k, :], k == 0, k == 1, *w_ok[j, k0], *gt_ok[j], *g_read.get(u - 2, ()))
                res.append(p)
            up_done[j] = p
            i = n
            a = SC.add(lambda e: e.activation(SG[i][:, :], GP[n][:, :], ACT.Silu), res[0], *g_read.get(u - 2, ()))
            d = DVE.add(lambda e: e.tensor_tensor(HF[i][:, :], SG[i][:, :], UP[n][:, :], ALU.mult), a, res[1], *h_ok.get(u - 2, ()))
            g_read[u] = (a, d)

        def split_h(j, n):
            r = HR[j % 2][:, :, 2 * n:2 * n + 2, :]
            h_ok[2 * j + n] = split(r[:, 0], r[:, 1], HF[n][:, :].rearrange("p (f t) -> p f t", f=2), g_read[2 * j + n][1], h_free.get(j - 2))

        def down(j):
            dn = WF[j % 2][:, :, 2048:3072].rearrange("p a (f d) -> p a f d", f=4)
            O = PO[:, j % 2, :]
            for a_ in range(2):
                for fc in range(4):
                    p = mm3(O[:, C * a_:C * a_ + C], lambda a, fc=fc, a_=a_: HR[j % 2][:, a, fc, 128 * a_:128 * a_ + 128], lambda a, fc=fc: dn[:, a, fc, :],
                            fc == 0, fc == 3, *w_ok[j, 2], *h_ok[2 * j], *h_ok[2 * j + 1], o_read.get(j - 2))
            h_free[j] = w_free[j] = p
            for a_ in range(2):
                t = SC.add(lambda e, a_=a_: e.activation(Y[j % 2][:, a_, :], O[:, C * a_:C * a_ + C], ACT.Copy, scale=TK[:, j, a_, 1:2]),
                           p, (s_add, 32 * (j - 1)) if j > 1 else None)
            o_read[j] = t
            for a_ in range(2):
                PL.dma(lambda e, a_=a_: e.indirect_dma_start(outr, bass.IndirectOffsetOnAxis(ap=TK[:, j, a_, 0:1].bitcast(i32), axis=0),
                                                             Y[j % 2][:, a_, :], None, bounds_check=TN - 1, oob_is_err=False, compute_op=ALU.add),
                       s_add, 32 * j + 16 * (a_ + 1), t, *out_ok.values(), (s_add, 32 * j) if j else None)

        fetched = [0]

        def beside_turn(upto):
            turn(NU + 3)
            while waiting and ready(waiting[0][0]):
                load_w(*waiting.pop(0))
            while fetched[0] <= min(upto, NT - 1) and ready(fetched[0]):
                load_tk(fetched[0])
                load_xg(fetched[0])
                fetched[0] += 1

        for k in range(3):
            load_w(1, k)
        fetched[0] = 3
        split_w(0, 0)
        split_w(0, 1)
        turn_x(0)
        for j in range(NT):
            if j + 1 < NT and not ready(j + 1):
                finish(NU + 3, lambda: ready(j + 1))
            beside_turn(j + 3)
            split_w(j + 1, 0)
            up_half(j, 0)
            beside_turn(j + 3)
            if j + 1 < NT:
                turn_x(j + 1)
            beside_turn(j + 3)
            split_w(j + 1, 1)
            split_h(j, 0)
            beside_turn(j + 3)
            up_half(j, 1)
            beside_turn(j + 3)
            split_w(j, 2)
            split_h(j, 1)
            beside_turn(j + 3)
            if j:
                down(j - 1)
            beside_turn(j + 3)
        down(NT - 1)
        SP.ops.append(("wait", s_add, 32 * NT))
        for r in (*sc_ok.values(), *out_ok.values(), *xd_ok.values()):
            SP.ops.append(("wait", *r))

        block = ctx.enter_context(nc.Block())

        @block.sync
        def _(eng):
            SP.play(eng)

        @block.tensor
        def _(eng):
            PE.play(eng)

        @block.vector
        def _(eng):
            DVE.play(eng)

        @block.scalar
        def _(eng):
            SC.play(eng)

        @block.gpsimd
        def _(eng):
            PL.play(eng)


def _lay(inputs):
    g = {k: np.asarray(v) for k, v in inputs.items()}
    wg = g["L0_ffn_w_gate"].transpose(0, 2, 1).reshape(NE, 2, 128, F).transpose(0, 2, 1, 3).reshape(NE, 128, 2 * F)
    wu = g["L0_ffn_w_up"].transpose(0, 2, 1).reshape(NE, 2, 128, F).transpose(0, 2, 1, 3).reshape(NE, 128, 2 * F)
    wn = g["L0_ffn_w_down"].transpose(0, 2, 1).reshape(NE, 4, 128, C).transpose(0, 2, 1, 3).reshape(NE, 128, 4 * C)
    a = {
        "x": g["x"], "ctxin": g["ctx_1024"],
        "lw": g["L0_attn_latent_w"].reshape(2, 128, L).transpose(1, 0, 2),
        "lb": g["L0_attn_latent_b"],
        "wd": g["L0_attn_Wd_w"].reshape(H, 2, 128, L).transpose(2, 1, 0, 3),
        "wdb": g["L0_attn_Wd_b"].T,
        "ow": g["L0_attn_out_w"].reshape(H, L, C).transpose(1, 0, 2),
        "ob": g["L0_attn_out_b"],
        "xw": g["L0_xattn_w"].reshape(2, 128).T,
        "xu": g["L0_xattn_u"].reshape(2, 128).T,
        "rw": g["L0_ffn_router_w"].T.reshape(2, 128, NE).transpose(1, 0, 2).reshape(128, 2 * NE),
        "wf": np.concatenate([wg, wu, wn], axis=2),
    }
    return {k: np.ascontiguousarray(v) for k, v in a.items()}


def kernel(**inputs):
    import concourse.bacc as bacc
    from concourse.bass_utils import run_bass_kernel_spmd as run

    nc = bacc.Bacc("TRN2", target_bir_lowering=False, num_devices=1)
    arrays = _lay(inputs)
    args = {n: nc.dram_tensor(n, a.shape, mybir.dt.from_np(a.dtype), kind="ExternalInput").ap() for n, a in arrays.items()}
    out = nc.dram_tensor("out", (B, T, C), mybir.dt.float32, kind="ExternalOutput").ap()
    xs = nc.dram_tensor("xs", (NE * CAP, 2), mybir.dt.float32, kind="Internal").ap()
    xd = nc.dram_tensor("xd", (TN + 1, C), mybir.dt.float32, kind="Internal").ap()
    build(nc, **args, out=out, xs=xs, xd=xd)
    r = run(nc, [arrays], core_ids=[0])
    return r.results[0]["out"]
```
